# Optimizing a Trainium2 kernel written in Bass

```python
import numpy as np
import jax
import jax.numpy as jnp

def _softmax(x, axis=-1):
    return jax.nn.softmax(x, axis=axis)

def _gelu(x):
    return jax.nn.gelu(x, approximate=True)

def _silu(x):
    return jax.nn.silu(x)

def _sigmoid(x):
    return jax.nn.sigmoid(x)

def _layernorm(x, axis=-1, eps=1e-05):
    m = jnp.mean(x, axis=axis, keepdims=True)
    v = jnp.var(x, axis=axis, keepdims=True)
    return (x - m) / jnp.sqrt(v + eps)

def _scatter_add(tgt, idx, src, axis=0):
    return tgt.at[idx].add(src)

def _segment_sum(src, seg, n):
    return jax.ops.segment_sum(src, seg, n)
kernel_name = 'mk_macaron_d1_jaxref_r8_190ac3'

def setup_inputs(seed: int=0):
    np.random.seed(seed)
    _w = jnp.asarray

    def _L0_attn_setup():
        import jax, jax.numpy as jnp
        import numpy as np
        B, S, H, NH = (1, 512, 128, 16)
        DH = H // NH

        def _split_heads(x):
            b, s, h = x.shape
            return jnp.transpose(x.reshape(b, s, NH, DH), (0, 2, 1, 3))
        key = jax.random.key(seed)
        ks = jax.random.split(key, 9)
        sc = 0.02
        return {'queries': jax.random.normal(ks[0], (B, S, H), jnp.float32), 'keys': jax.random.normal(ks[1], (B, S, H), jnp.float32), 'values': jax.random.normal(ks[2], (B, S, H), jnp.float32), 'Wq_w': jax.random.normal(ks[3], (H, H), jnp.float32) * sc, 'Wq_b': jax.random.normal(ks[4], (H,), jnp.float32) * sc, 'Wk_w': jax.random.normal(ks[5], (H, H), jnp.float32) * sc, 'Wk_b': jax.random.normal(ks[6], (H,), jnp.float32) * sc, 'Wv_w': jax.random.normal(ks[7], (H, H), jnp.float32) * sc, 'Wv_b': jax.random.normal(ks[8], (H,), jnp.float32) * sc}
    _L0_attn_in = _L0_attn_setup()

    def _L0_ffn_setup():
        import jax, jax.numpy as jnp
        import numpy as np
        EPS = 1e-05
        LN_EPS = 1e-05
        NUM_EXPERTS = 8
        TOP_K = 2
        HIDDEN = 128
        INTER = 256

        def _swiglu(x, wg, wu, wd):
            return jax.nn.silu(x @ wg) * (x @ wu) @ wd
        key = jax.random.key(seed)
        ks = jax.random.split(key, 10)
        B, S, H, I, E = (8, 512, HIDDEN, INTER, NUM_EXPERTS)
        std_h = 1.0 / np.sqrt(H)
        std_i = 1.0 / np.sqrt(I)
        return {'x': jax.random.normal(ks[0], (B, S, H), dtype=jnp.float32), 'ln_scale': jnp.ones((H,), dtype=jnp.float32), 'ln_bias': jnp.zeros((H,), dtype=jnp.float32), 'gate_w': jax.random.normal(ks[1], (E, H), dtype=jnp.float32) * 0.01, 'Wg': jax.random.normal(ks[2], (E, H, I), dtype=jnp.float32) * std_h, 'Wu': jax.random.normal(ks[3], (E, H, I), dtype=jnp.float32) * std_h, 'Wd': jax.random.normal(ks[4], (E, I, H), dtype=jnp.float32) * std_i, 'sWg': jax.random.normal(ks[5], (H, I), dtype=jnp.float32) * std_h, 'sWu': jax.random.normal(ks[6], (H, I), dtype=jnp.float32) * std_h, 'sWd': jax.random.normal(ks[7], (I, H), dtype=jnp.float32) * std_i}
    _L0_ffn_in = _L0_ffn_setup()
    _d = {'L0_attn_queries': _L0_attn_in['queries'], 'L0_attn_keys': _L0_attn_in['keys'], 'L0_attn_values': _L0_attn_in['values'], 'L0_attn_Wq_w': _L0_attn_in['Wq_w'], 'L0_attn_Wq_b': _L0_attn_in['Wq_b'], 'L0_attn_Wk_w': _L0_attn_in['Wk_w'], 'L0_attn_Wk_b': _L0_attn_in['Wk_b'], 'L0_attn_Wv_w': _L0_attn_in['Wv_w'], 'L0_attn_Wv_b': _L0_attn_in['Wv_b'], 'L0_ffn_ln_scale': _L0_ffn_in['ln_scale'], 'L0_ffn_ln_bias': _L0_ffn_in['ln_bias'], 'L0_ffn_gate_w': _L0_ffn_in['gate_w'], 'L0_ffn_Wg': _L0_ffn_in['Wg'], 'L0_ffn_Wu': _L0_ffn_in['Wu'], 'L0_ffn_Wd': _L0_ffn_in['Wd'], 'L0_ffn_sWg': _L0_ffn_in['sWg'], 'L0_ffn_sWu': _L0_ffn_in['sWu'], 'L0_ffn_sWd': _L0_ffn_in['sWd']}
    _x0 = _d['L0_attn_queries']
    _d['L0_attn_queries'] = jax.random.normal(jax.random.fold_in(jax.random.key(seed), 1), (16, 256, 128), dtype=_x0.dtype)
    del _x0
    return _d

def reference(L0_attn_queries, L0_attn_keys, L0_attn_values, L0_attn_Wq_w, L0_attn_Wq_b, L0_attn_Wk_w, L0_attn_Wk_b, L0_attn_Wv_w, L0_attn_Wv_b, L0_ffn_ln_scale, L0_ffn_ln_bias, L0_ffn_gate_w, L0_ffn_Wg, L0_ffn_Wu, L0_ffn_Wd, L0_ffn_sWg, L0_ffn_sWu, L0_ffn_sWd):

    def _L0_attn_ref(queries, keys, values, Wq_w, Wq_b, Wk_w, Wk_b, Wv_w, Wv_b):
        import jax, jax.numpy as jnp
        import numpy as np
        B, S, H, NH = (1, 512, 128, 16)
        DH = H // NH

        def _split_heads(x):
            b, s, h = x.shape
            return jnp.transpose(x.reshape(b, s, NH, DH), (0, 2, 1, 3))
        q = jax.nn.relu(queries @ Wq_w.T + Wq_b)
        k = jax.nn.relu(keys @ Wk_w.T + Wk_b)
        v = jax.nn.relu(values @ Wv_w.T + Wv_b)
        qh, kh, vh = (_split_heads(q), _split_heads(k), _split_heads(v))
        score = jnp.einsum('bhsd,bhtd->bhst', qh, kh) / jnp.sqrt(jnp.float32(DH))
        attn = jax.nn.softmax(score, axis=-1)
        a = jnp.einsum('bhst,bhtd->bhsd', attn, vh)
        a = jnp.transpose(a, (0, 1, 3, 2)).reshape(q.shape[0], q.shape[1], q.shape[2])
        return a + queries

    def _L0_ffn_ref(x, ln_scale, ln_bias, gate_w, Wg, Wu, Wd, sWg, sWu, sWd):
        import jax, jax.numpy as jnp
        import numpy as np
        EPS = 1e-05
        LN_EPS = 1e-05
        NUM_EXPERTS = 8
        TOP_K = 2
        HIDDEN = 128
        INTER = 256

        def _swiglu(x, wg, wu, wd):
            return jax.nn.silu(x @ wg) * (x @ wu) @ wd
        B, S, H = x.shape
        xf = x.reshape(-1, H)
        mu = jnp.mean(xf, axis=-1, keepdims=True)
        var = jnp.var(xf, axis=-1, keepdims=True)
        xn = (xf - mu) * jax.lax.rsqrt(var + LN_EPS) * ln_scale + ln_bias
        logits = xn @ gate_w.T
        probs = jax.nn.softmax(logits, axis=-1)
        tk_probs, tk_idx = jax.lax.top_k(probs, TOP_K)
        tk_probs = tk_probs / (jnp.sum(tk_probs, axis=-1, keepdims=True) + EPS)
        onehot = tk_idx[..., None] == jnp.arange(NUM_EXPERTS)[None, None, :]
        w = jnp.sum(tk_probs[..., None] * onehot.astype(tk_probs.dtype), axis=1)
        out = _swiglu(xf, sWg, sWu, sWd)
        for e in range(NUM_EXPERTS):
            out = out + w[:, e:e + 1] * _swiglu(xf, Wg[e], Wu[e], Wd[e])
        return out.reshape(B, S, H)
    x = L0_attn_queries
    x = x + 0.5 * _L0_ffn_ref(_layernorm(x, axis=-1), L0_ffn_ln_scale, L0_ffn_ln_bias, L0_ffn_gate_w, L0_ffn_Wg, L0_ffn_Wu, L0_ffn_Wd, L0_ffn_sWg, L0_ffn_sWu, L0_ffn_sWd)
    x = x + _L0_attn_ref(_layernorm(x, axis=-1), L0_attn_keys, L0_attn_values, L0_attn_Wq_w, L0_attn_Wq_b, L0_attn_Wk_w, L0_attn_Wk_b, L0_attn_Wv_w, L0_attn_Wv_b)
    x = x + 0.5 * _L0_ffn_ref(_layernorm(x, axis=-1), L0_ffn_ln_scale, L0_ffn_ln_bias, L0_ffn_gate_w, L0_ffn_Wg, L0_ffn_Wu, L0_ffn_Wd, L0_ffn_sWg, L0_ffn_sWu, L0_ffn_sWd)
    return x

_drawn_inputs = setup_inputs


def setup_inputs(seed=0):
    import zlib

    import numpy as np

    out = dict(_drawn_inputs(seed))
    spreads = {'L0_ffn_ln_scale': (1.0, 0.2), 'L0_ffn_ln_bias': (0.0, 0.1)}
    factors = {'L0_attn_keys': 8.0,
     'L0_attn_values': 8.0,
     'L0_attn_Wq_w': 8.0,
     'L0_attn_Wq_b': 8.0,
     'L0_attn_Wk_w': 8.0,
     'L0_attn_Wk_b': 45.811,
     'L0_attn_Wv_w': 8.0,
     'L0_attn_Wv_b': 40.284}
    for name, (base, spread) in spreads.items():
        noise = np.random.default_rng([zlib.crc32(name.encode()), seed]).standard_normal(out[name].shape)
        drawn = base * np.exp(spread * noise) if base else spread * noise
        out[name] = jnp.asarray(drawn.astype(out[name].dtype))
    for name, factor in factors.items():
        out[name] = (out[name] * factor).astype(out[name].dtype)
    return out
```

```python
from contextlib import ExitStack

import numpy as np

import concourse.bass as bass
from concourse import mybir

F32 = mybir.dt.float32
F32R = mybir.dt.float32r
ALU = mybir.AluOpType
ACT = mybir.ActivationFunctionType
AX = mybir.AxisListType

P = 128
NB, S, H = 16, 256, 128
KEYS, NH, DH = 512, 16, 8
NE, TOPK, INTER = 8, 2, 256
LN_EPS, TOPK_EPS = 1e-5, 1e-5
GT = 4
GTOK = GT * P
NG = NB * S // GTOK
EXP = NE + 1
STEPS = 2 * EXP
KB = KEYS // P
HI, HJ = 4, 4
WCOLS = 2 * INTER + 2 * H
LAG = 3
PRE = 6
RAW = 3
QROWS = 96
LN_VAR = 7
RT, RT_EXP = 21, 6
RING_KINDS = ("S", "PROJ", "YT", "MT")
IN_C, IN_K = 7 * 16, 8 * 16
POOL_SETS = 9
PLACED = 16 * 16


def build(nc, d):
    with ExitStack() as ctx:
        def sb(name, shape, dt=F32):
            return ctx.enter_context(nc.sbuf_tensor(name, shape, dt))

        def sem(name):
            return ctx.enter_context(nc.semaphore(name))

        psum = ctx.enter_context(nc.psum_tensor("psum", [P, 8, 512], F32))

        x = sb("x", [P, NG, GTOK])
        ident = sb("ident", [P, P])
        w_hi = sb("w_hi", [P, EXP, WCOLS], F32R)
        w_lo = sb("w_lo", [P, EXP, WCOLS], F32R)
        k_stack = sb("k_stack", [P, HI, HJ, KEYS], F32R)
        v_pad = sb("v_pad", [P, KB, HI, HJ, 32])
        minus_half = sb("minus_half", [P, GT])
        mean = sb("mean", [P, GT])
        mean2 = sb("mean2", [P, GT])
        stats = sb("stats", [P, GT, 6])
        ln_tmp = sb("ln_tmp", [P, 5, GT])
        var_eps = sb("var_eps", [P, GT])
        rstd = sb("rstd", [P, GT])
        rstd2 = sb("rstd2", [P, GT])
        z = sb("z", [P, GT, H])
        zT = sb("zT", [P, GTOK])
        work = sb("work", [P, 6, GTOK])
        w_raw = work[:].rearrange("p a n -> p (a n)")[:, 0:RAW * WCOLS].rearrange("p (r c) -> p r c", r=RAW)
        zT_hi = sb("zT_hi", [P, 2, GTOK], F32R)
        zT_lo = sb("zT_lo", [P, 2, GTOK], F32R)
        gate_t = sb("gate_t", [P, NE])
        ln_scale = sb("ln_scale", [P, 1])
        ln_bias = sb("ln_bias", [P, 1])
        gate_s = sb("gate_s", [P, 2, NE])
        gate_sum = sb("gate_sum", [P, 2, NE])
        ones = sb("ones", [P, P])
        euler = sb("euler", [P, GT, NE])
        lower = sb("lower", [P, NE, NE])
        expert_ind = sb("expert_ind", [P, NE])
        expert_sel = sb("expert_sel", [P, NE, P], F32R)
        r_a = sb("r_a", [P, GT, NE])
        r_b = sb("r_b", [P, GT, NE])
        r_c = sb("r_c", [P, GT, NE])
        r_exp = sb("r_exp", [P, GT, NE])
        r_1 = sb("r_1", [P, GT])
        r_2 = sb("r_2", [P, GT])
        r_3 = sb("r_3", [P, GT])
        r_gt = sb("r_gt", [P, GT, NE, NE])
        r_eq = sb("r_eq", [P, GT, NE, NE])
        route = sb("route", [P, GT, P], F32R)
        route_T = sb("route_T", [P, 2, GTOK], F32R)
        silu, act_up, h = work[:, 0:2, :], work[:, 2, :], work[:, 3:3 + LAG, :]
        h_hi = sb("h_hi", [P, LAG, GTOK], F32R)
        h_lo = sb("h_lo", [P, LAG, GTOK], F32R)
        out_T = sb("out_T", [P, GTOK])
        wq_raw = sb("wq_raw", [P, HI, QROWS])
        wq_hi = sb("wq_hi", [P, HI, QROWS], F32R)
        wq_lo = sb("wq_lo", [P, HI, QROWS], F32R)
        wk = sb("wk", [P, HI, QROWS])
        wvT = sb("wvT", [P, H])
        bq = sb("bq", [QROWS, HI])
        bk = sb("bk", [QROWS, HI])
        bv = sb("bv", [P, H])
        head_ind = sb("head_ind", [P, HJ])
        q_stack = sb("q_stack", [P, HI, GTOK], F32R)
        k_parts = q_stack
        yT_hi, yT_lo = zT_hi[:, 0, :], zT_lo[:, 0, :]
        q_fp = work[0:QROWS, 0:2, :]
        neg_max = sb("neg_max", [P, 2, GT, HJ])
        max_stage = sb("max_stage", [P, GT, P], F32R)
        probs = sb("probs", [P, 2, HJ, GTOK])
        k_fp, keysT, valuesT = probs[0:QROWS, 0, :, :], probs[:, 1, 0, :], probs[:, 1, 1, :]
        v_fp = probs[:, 1, 2, :].rearrange("p (k c) -> p k c", k=KB)
        acc_a, acc_b, num, den = (work[:, n, :] for n in range(2, 6))
        rden = out_T[:]

        in_c, in_k = sem("in_consts"), sem("in_attention")
        in_x = [sem(f"in_x{g}") for g in range(NG)]
        in_w = [sem(f"in_w{r}") for r in range(RAW)]
        gates_scaled, ones_set, pool_set, sel_set = sem("gates_scaled"), sem("ones_set"), sem("pool_set"), sem("sel_set")
        w_rounded, w_split = sem("w_rounded"), sem("w_split")
        k_projected, v_projected, gates_summed = sem("k_projected"), sem("v_projected"), sem("gates_summed")
        k_ready, k_rounded, k_split, k_stacked = sem("k_ready"), sem("k_rounded"), sem("k_split"), sem("k_stacked")
        wq_rounded, wq_split, v_ready, v_padded, sums_read = (sem("wq_rounded"), sem("wq_split"), sem("v_ready"),
                                                              sem("v_padded"), sem("sums_read"))
        ln_stat, ln_var, ln_rstd, ln_done = sem("ln_stat"), sem("ln_var"), sem("ln_rstd"), sem("ln_done")
        ln_stat2, ln_var2, ln_rstd2 = sem("ln_stat2"), sem("ln_var2"), sem("ln_rstd2")
        z_turned, z_copied, z_rounded, z_split = sem("z_turned"), sem("z_copied"), sem("z_rounded"), sem("z_split")
        logits_ready, rt_step, exp_ready = sem("logits_ready"), sem("rt_step"), sem("exp_ready")
        route_turned, route_copied = sem("route_turned"), sem("route_copied")
        gate_ready, up_ready, bc_ready, down_done = sem("gate_ready"), sem("up_ready"), sem("bc_ready"), sem("down_done")
        silu_ready, up_used, h_ready = sem("silu_ready"), sem("up_used"), sem("h_ready")
        hi_ready, lo_ready = sem("hi_ready"), sem("lo_ready")
        out_copied, out_turned, x_updated = sem("out_copied"), sem("out_turned"), sem("x_updated")
        s_filled, s_freed = sem("s_filled"), sem("s_freed")
        m_filled, m_freed = sem("m_filled"), sem("m_freed")
        q_rounded, q_ready = sem("q_rounded"), sem("q_ready")
        y_rounded, y_split, y_added = sem("y_rounded"), sem("y_split"), sem("y_added")
        max_hi, max_lo = sem("max_hi"), sem("max_lo")
        av_done, acc_copied, placed = sem("av_done"), sem("acc_copied"), sem("placed")
        recip_done, att_done, x_attended = sem("recip_done"), sem("att_done"), sem("x_attended")
        stored = sem("stored")

        G_BANK, U_BANK, BC_BANK, OUT_BANK, Z_BANK, R_BANK = (0, 1), (2, 3), 4, 5, 6, 7
        S_BANK, A_BANK, B_BANK, M_BANK = (0, 2), 4, 5, (6, 7)
        KP_BANK, VP_BANK, GS_BANK = (0, 1, 2, 3), 4, 5

        def bank(b, rows=P):
            return psum[0:rows, b, :]

        def of_group(buf, g):
            return buf[:, bass.ds(g, 1), :].rearrange("p a n -> p (a n)")

        block = ctx.enter_context(nc.Block())

        def ffn_windows(eng, window):
            window(0, 0, PRE, False)
            with eng.Fori(0, NG - 1) as g:
                window(g, PRE, PRE + STEPS, False)
            window(NG - 1, PRE, STEPS, True)

        def group_step(g, k):
            return (g + 1, k - STEPS) if k >= STEPS else (g, k)

        AT_STATS, AT_NORM, AT_TURN, AT_COPY, AT_SPLIT, AT_LOGITS, AT_ROUTE = 6, 7, 9, 10, 11, 12, 13
        AT_ROUTE_TURN, AT_ROUTE_COPY = 16, 17
        AT_OUT, AT_OUT_TURN, AT_UPDATE = STEPS + LAG, STEPS + LAG + 1, STEPS + LAG + 2

        def att_events(k, last):
            dg, r = divmod(k, HI * KB)
            i, kb = divmod(r, KB)
            u = HI * dg + i
            ahead = u + (2 if kb == KB - 1 else 1)
            out = [("S", u, kb, 0)]
            if not (last and ahead >= HI):
                out += [("M", ahead, (kb + 1) % GT, 0)]
            out += [("S", u, kb, 1)]
            if not (last and ahead >= HI):
                out += [("M", ahead, (kb + 1) % GT, 1)]
            out += [("AV", k - 1)]
            if kb == 0 and not (last and u + 2 >= HI):
                out += [("PROJ", u + 2)]
            if i == 1 and not last:
                out += {1: [("LN", dg + 1)], 2: [("YT", dg + 1, 0), ("YT", dg + 1, 1)]}.get(kb, [])
            if kb == KB - 1 and not (last and u + 1 >= HI):
                out += [("MT", u + 1)]
            if kb == 0 and i in (0, 2):
                out += [("EVAC", 2 * dg + i // 2 - 1)]
            if kb == KB - 1 and i == 0:
                out += [("POST", dg - 1)]
            return out

        def number(events, start):
            out = []
            for ev in events:
                out.append((*ev, start) if ev[0] in RING_KINDS else ev)
                start += ev[0] in RING_KINDS
            return out

        STEP0 = KB
        opening = [("LN", 0), ("YT", 0, 0), ("YT", 0, 1), ("PROJ", 0), ("PROJ", 1)]
        opening += [("M", 0, qt, half) for qt in range(GT) for half in range(2)]
        opening += [("MT", 0), ("M", 1, 0, 0), ("M", 1, 0, 1)]
        opening += [e for k in range(STEP0) for e in att_events(k, False)
                    if not (e[0] in ("AV", "EVAC", "POST") and e[1] < 0)]
        RING0 = sum(e[0] in RING_KINDS for e in opening)
        opening = number(opening, -RING0)
        middle = number([e for k in range(STEP0, STEP0 + HI * KB) for e in att_events(k, False)], 0)
        RING = sum(e[0] in RING_KINDS for e in middle)
        final = [e for k in range(STEP0, HI * KB) for e in att_events(k, True)]
        final = number(final + [("AV", HI * KB - 1), ("EVAC", 1), ("POST", 0)], 0)
        RING_END = sum(e[0] in RING_KINDS for e in final)
        assert RING % 2 == 0

        def ring_uses(events):
            mt, sc = {}, {}
            for ev in opening + (events if events is not opening else []):
                if ev[0] == "MT":
                    mt[ev[1]] = ev[-1]
                if ev[0] == "S" and ev[3] == 1:
                    sc[ev[1] * KB + ev[2]] = ev[-1]
            return mt, sc

        def ring_bank(use):
            return S_BANK[(RING0 + use) % 2]

        def att_windows(eng, window):
            window(0, opening)
            with eng.Fori(0, NG - 1) as g:
                window(g, middle)
            window(NG - 1, final)

        @block.sync
        def _(sp):
            def load_x(g):
                sp.dma_start(x[:, g, :].rearrange("p (b n) -> p b n", b=2),
                             d["x"][2 * g:2 * g + 2].rearrange("b (p t) f -> p b (t f)", t=2)).then_inc(in_x[g], 16)

            def load_expert(e):
                if e >= RAW:
                    sp.wait_ge(w_split, e - RAW + 1)
                wg, wu, wd = (d["sWg"], d["sWu"], d["sWd"]) if e == 0 else (d["Wg"][e - 1], d["Wu"][e - 1], d["Wd"][e - 1])
                r = e % RAW
                sp.dma_start(w_raw[:, r, 0:INTER], wg).then_inc(in_w[r], 16)
                sp.dma_start(w_raw[:, r, INTER:2 * INTER], wu).then_inc(in_w[r], 16)
                sp.dma_start(w_raw[:, r, 2 * INTER:].rearrange("p (i n) -> p i n", i=2),
                             wd.rearrange("(i p) n -> p i n", i=2)).then_inc(in_w[r], 16)

            load_x(0)
            for to, of in ((ident[:], "c_ident"), (expert_ind[:], "c_expert"), (lower[:].rearrange("p e f -> p (e f)"), "c_lower"),
                           (head_ind[:], "c_head"), (gate_t[:], "gate_t"), (ln_scale[:], "ln_scale"), (ln_bias[:], "ln_bias")):
                sp.dma_start(to, d[of]).then_inc(in_c, 16)
            for e in range(EXP):
                load_expert(e)
                if e == RAW - 1:
                    load_x(1)
            for g in range(2, NG):
                load_x(g)

            half = 2 * DH
            def place(g):
                sp.wait_ge(acc_copied, 2 * g + 2)
                sp.wait_ge(att_done, g)
                for to, of, t0, f0 in ((num, acc_a, 0, 0), (num, acc_b, half, 0), (den, acc_a, 0, half), (den, acc_b, half, half)):
                    for j in range(HJ):
                        sp.dma_start(to[32 * j + t0:32 * j + t0 + half, :],
                                     of[32 * j + f0:32 * j + f0 + half, :]).then_inc(placed, 16)

            with sp.Fori(0, NG) as g:
                place(g)
            with sp.Fori(0, NG) as g:
                sp.wait_ge(x_updated, g + (NG + 1))
                for b in range(2):
                    sp.dma_start(d["out"][bass.ds(2 * g + b, 1)].rearrange("b (p t) f -> (b p) (t f)", t=2),
                                 x[:, bass.ds(g, 1), b * S:(b + 1) * S].rearrange("p a n -> p (a n)")).then_inc(stored, 16)
            sp.wait_ge(stored, 16 * NB)

        @block.tensor
        def _(pe):
            mm = nc.tensor.matmul

            def three(out, w, wl, m, ml, start, stop):
                mm(out, w, m, start=start, stop=False)
                mm(out, w, ml, start=False, stop=False)
                return mm(out, wl, m, start=False, stop=stop)

            def turn(out, in_):
                return nc.tensor.transpose(out, in_, ident[:])

            pe.wait_ge(in_c, IN_C)
            pe.wait_ge(ones_set, 1)
            pe.wait_ge(gates_scaled, 2)
            mm(psum[:, GS_BANK, 0:2 * NE], ones[:], gate_s[:].rearrange("p a e -> p (a e)"),
               start=True, stop=True).then_inc(gates_summed, 1)
            pe.wait_ge(in_k, IN_K)
            for i in range(HI):
                mm(bank(KP_BANK[i], QROWS), wk[:, i, :], keysT, start=True, stop=True).then_inc(k_projected, 1)
            for kb in range(KB):
                last = mm(psum[:, VP_BANK, kb * H:(kb + 1) * H], valuesT[:, kb * P:(kb + 1) * P], wvT[:],
                          start=True, stop=True)
            last.then_inc(v_projected, 1)

            def ffn(ph):
                base, groups = ph * NG * STEPS, ph * NG

                def prep_z(g):
                    pe.wait_ge(ln_done, g + 2 * groups + 1)
                    if not (isinstance(g, int) and g == 0):
                        pe.wait_ge(x_updated, g + groups - 1)
                    for t in range(GT):
                        last = turn(psum[:, Z_BANK, t * P:(t + 1) * P], z[:, t, :])
                    last.then_inc(z_turned, 1)

                def prep_logits(g):
                    pe.wait_ge(z_copied, g + groups + 1)
                    pe.wait_ge(route_copied, g + groups)
                    for t in range(GT):
                        last = mm(psum[:, R_BANK, t * NE:(t + 1) * NE], zT[:, t * P:(t + 1) * P], gate_s[:, 0, :],
                                  start=True, stop=True)
                    last.then_inc(logits_ready, 1)

                def prep_route(g):
                    pe.wait_ge(rt_step, g * RT + (groups * RT + RT))
                    for t in range(GT):
                        last = turn(psum[:, R_BANK, t * P:(t + 1) * P], route[:, t, :].bitcast(F32))
                    last.then_inc(route_turned, 1)

                def gate_up(g, s):
                    n = g * STEPS + (s + base)
                    e, i = divmod(s, 2)
                    opens = ph == 0 and isinstance(g, int) and g == 0 and s < 2
                    zh, zl = of_group(zT_hi, g % 2), of_group(zT_lo, g % 2)
                    if s == 0:
                        pe.wait_ge(z_split, g + groups + 1)
                    if not opens:
                        pe.wait_ge(silu_ready, n - 1)
                    c = i * P
                    three(bank(G_BANK[s % 2]), w_hi[:, e, c:c + P], w_lo[:, e, c:c + P], zh, zl,
                          True, True).then_inc(gate_ready, 1)
                    if not opens:
                        pe.wait_ge(up_used, n - 1)
                    c = INTER + i * P
                    three(bank(U_BANK[s % 2]), w_hi[:, e, c:c + P], w_lo[:, e, c:c + P], zh, zl,
                          True, True).then_inc(up_ready, 1)

                def down(g, s):
                    n = g * STEPS + (s + base)
                    e, i = divmod(s, 2)
                    pe.wait_ge(lo_ready, n + 1)
                    if s == 0:
                        pe.wait_ge(out_copied, g + groups)
                    c = 2 * INTER + i * H
                    three(bank(OUT_BANK), w_hi[:, e, c:c + H], w_lo[:, e, c:c + H], h_hi[:, s % LAG, :],
                          h_lo[:, s % LAG, :], s == 0, s == STEPS - 1).then_inc(down_done, 1)

                def broadcast(g, s):
                    e = s // 2 - 1
                    if e == 0:
                        pe.wait_ge(route_copied, g + groups + 1)
                    pe.wait_ge(h_ready, g * (2 * NE) + (groups * 2 * NE + 2 * e))
                    mm(bank(BC_BANK), expert_sel[:, e, :], of_group(route_T, g % 2),
                       start=True, stop=True).then_inc(bc_ready, 1)

                def finish(g, last_group):
                    pe.wait_ge(out_copied, g + groups + 1)
                    pe.wait_ge(z_copied, g + groups + (1 if last_group else 2))
                    for t in range(GT):
                        last = turn(psum[:, Z_BANK, t * P:(t + 1) * P], out_T[:, t * P:(t + 1) * P])
                    last.then_inc(out_turned, 1)

                def window(g, k0, k1, last):
                    for k in range(k0, k1):
                        gg, s = group_step(g, k)
                        gate_up(gg, s)
                        if k >= LAG:
                            down(*group_step(g, k - LAG))
                        if s >= 2 and s % 2 == 0:
                            broadcast(gg, s)
                        if not last:
                            if k == AT_TURN:
                                prep_z(g + 1)
                            if k == AT_LOGITS:
                                prep_logits(g + 1)
                            if k == AT_ROUTE_TURN:
                                prep_route(g + 1)
                            if k == AT_OUT_TURN:
                                finish(g, False)
                    if last:
                        for k in range(STEPS - LAG, STEPS):
                            down(g, k)
                        finish(g, True)

                prep_z(0)
                prep_logits(0)
                prep_route(0)
                ffn_windows(pe, window)

            pe.wait_ge(k_ready, HI)
            pe.wait_ge(v_ready, 1)
            pe.wait_ge(sums_read, 1)
            pe.wait_ge(w_split, EXP)
            pe.wait_ge(sel_set, 1)
            ffn(0)

            pe.wait_ge(x_updated, NG)
            pe.wait_ge(silu_ready, NG * STEPS)
            pe.wait_ge(h_ready, NG * 2 * NE)
            pe.wait_ge(k_stacked, HJ)
            pe.wait_ge(wq_split, 1)
            pe.wait_ge(v_padded, HI)
            pe.wait_ge(pool_set, POOL_SETS)

            def attend(g0, events):
                mt_use, s_use = ring_uses(events)

                def claim(use):
                    if use >= 2 - RING0:
                        pe.wait_ge(s_freed, g0 * RING + (RING0 + use - 1))
                    return ring_bank(use)

                for ev in events:
                    kind, use = ev[0], ev[-1]
                    if kind == "S":
                        _, u, kb, jp, _ = ev
                        i = u % HI
                        if kb == 0 and jp == 0:
                            pe.wait_ge(s_freed, g0 * RING + (RING0 + mt_use[u] + 1))
                        b = claim(use)
                        for j in (2 * jp, 2 * jp + 1):
                            last = mm(bank(b + j % 2), k_stack[:, i, j, kb * P:(kb + 1) * P], q_stack[:, i, :],
                                      start=True, stop=True)
                        last.then_inc(s_filled, 1)
                    elif kind == "M":
                        _, u, qt, half = ev
                        i = u % HI
                        if qt == 0 and half == 0:
                            pe.wait_ge(q_ready, g0 * HI + (u + 1))
                        for j in (2 * half, 2 * half + 1):
                            r = 16 * u + 4 * qt + j
                            if r >= 2:
                                pe.wait_ge(m_freed, g0 * 64 + (r - 1))
                            mm(bank(M_BANK[j % 2]), q_stack[0:QROWS, i, qt * P:(qt + 1) * P], k_stack[0:QROWS, i, j, :],
                               start=True, stop=True).then_inc(m_filled, 1)
                    elif kind == "PROJ":
                        i = ev[1] % HI
                        if i == 0:
                            pe.wait_ge(y_split, g0 + (ev[1] // HI + 1))
                        three(bank(claim(use), QROWS), wq_hi[:, i, :], wq_lo[:, i, :], yT_hi, yT_lo,
                              True, True).then_inc(s_filled, 1)
                    elif kind == "YT":
                        _, dg, half, _ = ev
                        pe.wait_ge(ln_done, g0 + (dg + NG + 1))
                        b = claim(use)
                        for t in range(2):
                            last = turn(psum[:, b, t * P:(t + 1) * P], z[:, 2 * half + t, :])
                        last.then_inc(s_filled, 1)
                    elif kind == "MT":
                        pe.wait_ge(max_lo, g0 * HI + (ev[1] + 1))
                        b = claim(use)
                        for t in range(GT):
                            last = turn(psum[:, b, t * P:(t + 1) * P], max_stage[:, t, :].bitcast(F32))
                        last.then_inc(s_filled, 1)
                    elif kind == "AV":
                        k = ev[1]
                        dg, r = divmod(k, HI * KB)
                        i, kb = divmod(r, KB)
                        pe.wait_ge(s_freed, g0 * RING + (RING0 + s_use[k] + 1))
                        if kb == 0 and i % 2 == 0 and 2 * dg + i // 2 - 1 >= 0:
                            pe.wait_ge(acc_copied, g0 * 2 + (2 * dg + i // 2 - 1))
                        for j in range(HJ):
                            last = mm(psum[32 * j:32 * j + 32, A_BANK if i < 2 else B_BANK, :],
                                      v_pad[:, kb, i, j, :], probs[:, kb % 2, j, :],
                                      start=(i % 2 == 0 and kb == 0), stop=(i % 2 == 1 and kb == KB - 1))
                        last.then_inc(av_done, 1)

            att_windows(pe, attend)
            pe.wait_ge(s_freed, RING * (NG - 1) + RING0 + RING_END)
            pe.wait_ge(m_freed, 64 * NG)
            pe.wait_ge(acc_copied, 2 * NG)
            ffn(1)

        @block.scalar
        def _(act):
            for to, of in ((wk[:].rearrange("p i c -> p (i c)"), "wk"), (keysT, "keysT"), (wvT[:], "wvT"), (valuesT, "valuesT"),
                           (wq_raw[:].rearrange("p i c -> p (i c)"), "wq"), (bq[:], "bq"), (bk[:], "bk"), (bv[:], "bv")):
                act.dma_start(to, d[of]).then_inc(in_k, 16)
            act.wait_ge(in_k, IN_K)
            for i in range(HI):
                act.wait_ge(k_projected, i + 1)
                nc.scalar.activation(k_fp[:, i, :], bank(KP_BANK[i], QROWS), ACT.Relu, bias=bk[:, i:i + 1]).then_inc(k_ready, 1)
            for e in range(EXP):
                act.wait_ge(in_w[e % RAW], 48 * (e // RAW + 1))
                nc.scalar.copy(w_hi[:, e, :], w_raw[:, e % RAW, :]).then_inc(w_rounded, 1)

            def ffn(ph):
                base, groups = ph * NG * STEPS, ph * NG

                def copy_z(g):
                    act.wait_ge(z_turned, g + groups + 1)
                    act.wait_ge(z_split, g + groups)
                    act.wait_ge(logits_ready, g + groups)
                    nc.scalar.copy(zT[:], bank(Z_BANK)).then_inc(z_copied, 1)

                def copy_route(g):
                    act.wait_ge(route_turned, g + groups + 1)
                    nc.scalar.copy(of_group(route_T, g % 2), bank(R_BANK)).then_inc(route_copied, 1)

                def copy_out(g):
                    act.wait_ge(down_done, g * STEPS + (base + STEPS))
                    act.wait_ge(out_turned, g + groups)
                    nc.scalar.copy(out_T[:], bank(OUT_BANK)).then_inc(out_copied, 1)

                def gates(g, s):
                    n = g * STEPS + (s + base)
                    act.wait_ge(gate_ready, n + 1)
                    if not (ph == 0 and isinstance(g, int) and g == 0 and s < 2):
                        act.wait_ge(up_used, n - 1)
                    nc.scalar.activation(silu[:, s % 2, :], bank(G_BANK[s % 2]), ACT.Silu).then_inc(silu_ready, 1)

                def round_h(g, s):
                    n = g * STEPS + (s + base)
                    if s < 2:
                        act.wait_ge(up_used, n + 1)
                    else:
                        act.wait_ge(h_ready, g * (2 * NE) + (groups * 2 * NE + s - 1))
                    if not (ph == 0 and isinstance(g, int) and g == 0 and s < LAG):
                        act.wait_ge(down_done, n - (LAG - 1))
                    nc.scalar.copy(h_hi[:, s % LAG, :], h[:, s % LAG, :]).then_inc(hi_ready, 1)

                def window(g, k0, k1, last):
                    for k in range(k0, k1):
                        if k == AT_OUT:
                            copy_out(g)
                        gates(*group_step(g, k))
                        if k >= 1:
                            round_h(*group_step(g, k - 1))
                        if not last:
                            if k == AT_COPY:
                                copy_z(g + 1)
                            if k == AT_ROUTE_COPY:
                                copy_route(g + 1)
                    if last:
                        round_h(g, STEPS - 1)
                        copy_out(g)

                copy_z(0)
                copy_route(0)
                ffn_windows(act, window)

            ffn(0)

            def attend(g0, events):
                for ev in events:
                    kind, use = ev[0], ev[-1]
                    if kind in RING_KINDS:
                        act.wait_ge(s_filled, g0 * RING + (RING0 + use + 1))
                        b = ring_bank(use)
                    if kind == "S":
                        _, u, kb, jp, _ = ev
                        k = u * KB + kb
                        if k >= 2 and jp == 0:
                            act.wait_ge(av_done, g0 * 16 + (k - 1))
                        nc.scalar.activation(probs[:, kb % 2, 2 * jp:2 * jp + 2, :], psum[:, b:b + 2, :], ACT.Exp,
                                             scale=float(DH) ** -0.5).then_inc(s_freed, 1)
                    elif kind == "PROJ":
                        u = ev[1]
                        if u >= 2:
                            act.wait_ge(q_ready, g0 * HI + (u - 1))
                        nc.scalar.activation(q_fp[:, u % 2, :], bank(b, QROWS), ACT.Relu,
                                             bias=bq[:, u % HI:u % HI + 1]).then_inc(s_freed, 1)
                    elif kind == "YT":
                        _, dg, half, _ = ev
                        act.wait_ge(y_split, g0 + dg)
                        nc.scalar.copy(zT[:, 2 * half * P:2 * (half + 1) * P], psum[:, b, 0:2 * P]).then_inc(s_freed, 1)
                    elif kind == "MT":
                        nc.scalar.copy(q_stack[QROWS:P, ev[1] % HI, :], psum[QROWS:P, b, :]).then_inc(s_freed, 1)
                    elif kind == "EVAC":
                        n = ev[1]
                        act.wait_ge(av_done, g0 * 16 + 8 * (n + 1))
                        act.wait_ge(placed, g0 * PLACED + PLACED * (n // 2))
                        nc.scalar.copy(acc_b if n % 2 else acc_a, bank(B_BANK if n % 2 else A_BANK)).then_inc(acc_copied, 1)

            att_windows(act, attend)
            ffn(1)

        @block.vector
        def _(dve):
            tt, ts = nc.vector.tensor_tensor, nc.vector.tensor_scalar
            stt, cp = nc.vector.scalar_tensor_tensor, nc.vector.tensor_copy

            def spread(v, n):
                return v.unsqueeze(2).broadcast_to([P, GT, n])

            nc.vector.memset(ones[:], 1.0).then_inc(ones_set, 1)
            dve.wait_ge(in_c, IN_C)
            ts(gate_s[:, 0, :], gate_t[:], ln_scale[:], None, ALU.mult).then_inc(gates_scaled, 1)
            ts(gate_s[:, 1, :], gate_t[:], ln_bias[:], None, ALU.mult).then_inc(gates_scaled, 1)
            dve.wait_ge(ones_set, 1)
            for e in range(NE):
                last = ts(expert_sel[:, e, :], ones[:], expert_ind[:, e:e + 1], None, ALU.mult)
            last.then_inc(sel_set, 1)
            dve.wait_ge(gates_summed, 1)
            cp(gate_sum[:].rearrange("p a e -> p (a e)"), psum[:, GS_BANK, 0:2 * NE]).then_inc(sums_read, 1)
            dve.wait_ge(in_k, IN_K)
            cp(wq_hi[:], wq_raw[:]).then_inc(wq_rounded, 1)
            dve.wait_ge(wq_rounded, 1)
            tt(wq_lo[:], wq_raw[:], wq_hi[:].bitcast(F32), ALU.subtract).then_inc(wq_split, 1)
            nc.vector.memset(k_parts[QROWS:P, :, :].bitcast(F32), 1.0)
            for i in range(HI):
                dve.wait_ge(k_ready, i + 1)
                cp(k_parts[0:QROWS, i, :], k_fp[:, i, :]).then_inc(k_rounded, 1)
                dve.wait_ge(k_rounded, i + 1)
                tt(k_parts[32:64, i, :], k_fp[32:64, i, :], k_parts[32:64, i, :].bitcast(F32), ALU.subtract).then_inc(k_split, 1)
            dve.wait_ge(k_split, HI)
            for j in range(HJ):
                ts(k_stack[:, :, j, :], k_parts[:].bitcast(F32), head_ind[:, j:j + 1], None, ALU.mult).then_inc(k_stacked, 1)
            dve.wait_ge(v_projected, 1)
            tt(v_fp, bank(VP_BANK).rearrange("p (k c) -> p k c", k=KB), bv[:].unsqueeze(1).broadcast_to([P, KB, H]),
               ALU.add).then_inc(v_ready, 1)
            dve.wait_ge(v_ready, 1)
            dve.wait_ge(pool_set, POOL_SETS)
            v_heads = v_fp.rearrange("p k (j i c) -> p k i j c", i=HI, j=HJ)
            for i in range(HI):
                c = DH * (i % 2)
                ts(v_pad[:, :, i, :, c:c + DH], v_heads[:, :, i, :, :], 0.0, None, ALU.max).then_inc(v_padded, 1)
            for e in range(EXP):
                dve.wait_ge(w_rounded, e + 1)
                tt(w_lo[:, e, :], w_raw[:, e % RAW, :], w_hi[:, e, :].bitcast(F32), ALU.subtract).then_inc(w_split, 1)

            def moments(n, rows, stat_sem, var_sem, mean_out):
                for t in range(GT):
                    nc.vector.bn_stats(stats[:, t, :], rows[:, t * H:(t + 1) * H]).then_inc(stat_sem, 1)
                dve.wait_ge(stat_sem, n * GT + GT)
                mean_e, mean_o, m2_e, m2_o = (stats[:, :, c] for c in (1, 4, 2, 5))
                total, apart, apart2, m2, var = (ln_tmp[:, c, :] for c in range(5))
                tt(total, mean_e, mean_o, ALU.add).then_inc(var_sem, 1)
                tt(apart, mean_e, mean_o, ALU.subtract).then_inc(var_sem, 1)
                tt(m2, m2_e, m2_o, ALU.add).then_inc(var_sem, 1)
                dve.wait_ge(var_sem, n * LN_VAR + 3)
                ts(mean_out[:], total, 0.5, None, ALU.mult).then_inc(var_sem, 1)
                stt(out=apart2, in0=apart, scalar=0.25, in1=apart, op0=ALU.mult, op1=ALU.mult).then_inc(var_sem, 1)
                ts(var, m2, 1.0 / H, LN_EPS, ALU.mult, ALU.add).then_inc(var_sem, 1)
                dve.wait_ge(var_sem, n * LN_VAR + 6)
                tt(var_eps[:], var, apart2, ALU.add).then_inc(var_sem, 1)

            def norm_stats(n, g):
                moments(n, of_group(x, g), ln_stat, ln_var, mean)

            def norm(n, g):
                dve.wait_ge(ln_rstd, n + 1)
                for t in range(GT):
                    last = ts(z[:, t, :], of_group(x, g)[:, t * H:(t + 1) * H], mean[:, t:t + 1], rstd[:, t:t + 1],
                              ALU.subtract, ALU.mult)
                last.then_inc(ln_done, 1)

            def ffn(ph):
                base, groups = ph * NG * STEPS, ph * NG

                def prep_stats(g):
                    if ph == 0 and isinstance(g, int):
                        dve.wait_ge(in_x[g], 16)
                    if ph == 1:
                        dve.wait_ge(x_attended, 2 * g + 2)
                    norm_stats(g + 2 * groups, g)

                def prep_norm(g):
                    dve.wait_ge(z_turned, g + groups)
                    norm(g + 2 * groups, g)
                    n = g + groups
                    dve.wait_ge(ln_done, g + (2 * groups + 1))
                    moments(n, z[:].rearrange("p t f -> p (t f)"), ln_stat2, ln_var2, mean2)

                def prep_round(g):
                    dve.wait_ge(z_copied, g + groups + 1)
                    cp(of_group(zT_hi, g % 2), zT[:]).then_inc(z_rounded, 1)

                def prep_route(g):
                    n = g + groups
                    done = [0]

                    def link(ins):
                        done[0] += 1
                        ins.then_inc(rt_step, 1)
                        dve.wait_ge(rt_step, n * RT + done[0])

                    logits = psum[:, R_BANK, 0:GT * NE].rearrange("p (t e) -> p t e", t=GT)
                    dve.wait_ge(logits_ready, n + 1)
                    dve.wait_ge(ln_rstd2, n + 1)
                    link(tt(r_a[:], gate_sum[:, 0, :].unsqueeze(1).broadcast_to([P, GT, NE]), spread(mean2[:], NE), ALU.mult))
                    link(tt(r_b[:], logits, r_a[:], ALU.subtract))
                    link(tt(r_a[:], r_b[:], spread(rstd2[:], NE), ALU.mult))
                    link(tt(r_b[:], r_a[:], gate_sum[:, 1, :].unsqueeze(1).broadcast_to([P, GT, NE]), ALU.add))
                    link(nc.vector.tensor_reduce(r_1[:], r_b[:], AX.X, ALU.max))
                    link(tt(r_c[:], r_b[:], spread(r_1[:], NE), ALU.subtract))
                    assert done[0] == RT_EXP
                    dve.wait_ge(exp_ready, n + 1)
                    link(nc.vector.tensor_reduce(r_2[:], r_exp[:], AX.X, ALU.add))
                    link(nc.vector.reciprocal(r_3[:], r_2[:]))
                    link(tt(r_a[:], r_exp[:], spread(r_3[:], NE), ALU.mult))
                    of_f = r_a[:].unsqueeze(2).broadcast_to([P, GT, NE, NE])
                    of_e = r_a[:].unsqueeze(3).broadcast_to([P, GT, NE, NE])
                    link(tt(r_gt[:], of_f, of_e, ALU.is_gt))
                    link(tt(r_eq[:], of_f, of_e, ALU.is_equal))
                    link(tt(r_eq[:], r_eq[:], lower[:].unsqueeze(1).broadcast_to([P, GT, NE, NE]), ALU.mult))
                    link(tt(r_gt[:], r_gt[:], r_eq[:], ALU.add))
                    link(nc.vector.tensor_reduce(r_b[:], r_gt[:], AX.X, ALU.add))
                    link(stt(out=r_c[:], in0=r_b[:], scalar=float(TOPK), in1=r_a[:], op0=ALU.is_lt, op1=ALU.mult))
                    link(nc.vector.tensor_reduce(r_1[:], r_c[:], AX.X, ALU.add))
                    link(ts(r_2[:], r_1[:], TOPK_EPS, None, ALU.add))
                    link(nc.vector.reciprocal(r_3[:], r_2[:]))
                    link(tt(r_b[:], r_c[:], spread(r_3[:], NE), ALU.mult))
                    dve.wait_ge(route_turned, n)
                    link(cp(route[:, :, 0:NE], r_b[:]))
                    link(tt(route[:, :, 32:32 + NE], r_b[:], route[:, :, 0:NE].bitcast(F32), ALU.subtract))
                    assert done[0] == RT

                def product(g, s):
                    n = g * STEPS + (s + base)
                    dve.wait_ge(up_ready, n + 1)
                    dve.wait_ge(silu_ready, n + 1)
                    if not (ph == 0 and isinstance(g, int) and g == 0 and s < LAG):
                        dve.wait_ge(lo_ready, n - (LAG - 1))
                    if s < 2:
                        tt(h[:, s % LAG, :], silu[:, s % 2, :], bank(U_BANK[s % 2]), ALU.mult).then_inc(up_used, 1)
                    else:
                        dve.wait_ge(h_ready, g * (2 * NE) + (groups * 2 * NE + s - 2))
                        tt(act_up, silu[:, s % 2, :], bank(U_BANK[s % 2]), ALU.mult).then_inc(up_used, 1)
                        dve.wait_ge(bc_ready, g * NE + (groups * NE + s // 2))
                        dve.wait_ge(up_used, n + 1)
                        tt(h[:, s % LAG, :], act_up, bank(BC_BANK), ALU.mult).then_inc(h_ready, 1)

                def update(g):
                    dve.wait_ge(out_turned, g + groups + 1)
                    stt(out=of_group(x, g), in0=bank(Z_BANK), scalar=0.5, in1=of_group(x, g), op0=ALU.mult,
                        op1=ALU.add).then_inc(x_updated, 1)

                def window(g, k0, k1, last):
                    for k in range(k0, k1):
                        product(*group_step(g, k))
                        if not last:
                            if k == AT_STATS:
                                prep_stats(g + 1)
                            if k == AT_NORM:
                                prep_norm(g + 1)
                            if k == AT_SPLIT:
                                prep_round(g + 1)
                            if k == AT_ROUTE:
                                prep_route(g + 1)
                            if k == AT_UPDATE:
                                update(g)
                    if last:
                        update(g)

                prep_stats(0)
                prep_norm(0)
                prep_round(0)
                prep_route(0)
                if ph == 0:
                    for g in range(1, NG):
                        dve.wait_ge(in_x[g], 16)
                ffn_windows(dve, window)

            ffn(0)

            def attend(g0, events):
                mt_use, _ = ring_uses(events)
                for ev in events:
                    kind = ev[0]
                    if kind == "M":
                        _, u, qt, half = ev
                        for j in (2 * half, 2 * half + 1):
                            dve.wait_ge(m_filled, g0 * 64 + (16 * u + 4 * qt + j + 1))
                            nc.vector.tensor_reduce(neg_max[:, u % 2, qt, j:j + 1], bank(M_BANK[j % 2]), AX.X, ALU.max,
                                                    negate=True).then_inc(m_freed, 1)
                        if qt == GT - 1 and half == 1:
                            dve.wait_ge(m_freed, g0 * 64 + 16 * (u + 1))
                            if u >= 1:
                                dve.wait_ge(s_filled, g0 * RING + (RING0 + mt_use[u - 1] + 1))
                            cp(max_stage[:, :, QROWS:QROWS + HJ], neg_max[:, u % 2]).then_inc(max_hi, 1)
                            dve.wait_ge(max_hi, g0 * HI + (u + 1))
                            tt(max_stage[:, :, QROWS + HJ:QROWS + 2 * HJ], neg_max[:, u % 2],
                               max_stage[:, :, QROWS:QROWS + HJ].bitcast(F32), ALU.subtract).then_inc(max_lo, 1)
                    elif kind == "LN":
                        g = g0 + ev[1]
                        norm_stats(g + NG, g)
                        dve.wait_ge(y_added, g)
                        norm(g + NG, g)
                    elif kind == "POST":
                        g = g0 + ev[1]
                        dve.wait_ge(placed, g * PLACED + PLACED)
                        nc.vector.reciprocal(rden, den).then_inc(recip_done, 1)
                        dve.wait_ge(recip_done, g + 1)
                        tt(num, num, rden, ALU.mult).then_inc(att_done, 1)
                        dve.wait_ge(att_done, g + 1)
                        dve.wait_ge(y_added, g + 1)
                        for t in range(2):
                            xs = of_group(x, g).rearrange("p (b k t) -> p b k t", b=2, t=2)[:, :, :, t]
                            tt(xs, xs, num.rearrange("p (b t k) -> p b t k", b=2, t=2)[:, :, t, :], ALU.add).then_inc(x_attended, 1)

            att_windows(dve, attend)
            ffn(1)

        @block.gpsimd
        def _(pool):
            nc.gpsimd.memset(minus_half[:], -0.5).then_inc(pool_set, 1)
            nc.gpsimd.memset(euler[:], float(np.e)).then_inc(pool_set, 1)
            nc.gpsimd.memset(route[:].bitcast(F32), 0.0).then_inc(pool_set, 1)
            nc.gpsimd.memset(max_stage[:].bitcast(F32), 0.0).then_inc(pool_set, 1)
            nc.gpsimd.memset(v_pad[:], 0.0).then_inc(pool_set, 1)
            pool.wait_ge(pool_set, 5)
            for i in range(HI):
                c = 2 * DH + DH * (i % 2)
                nc.gpsimd.memset(v_pad[:, :, i, :, c:c + DH], 1.0).then_inc(pool_set, 1)
            pool.wait_ge(pool_set, POOL_SETS)

            def one_of(rows):
                return ones[0:rows, 0:1].broadcast_to([rows, GTOK])

            def inverse_root(n, var_sem, out, out_sem):
                pool.wait_ge(var_sem, n * LN_VAR + LN_VAR)
                nc.gpsimd.tensor_tensor(out[:], var_eps[:], minus_half[:], ALU.pow).then_inc(out_sem, 1)

            def ffn(ph):
                base, groups = ph * NG * STEPS, ph * NG

                def prep_stats(g):
                    inverse_root(g + 2 * groups, ln_var, rstd, ln_rstd)

                def prep_norm(g):
                    inverse_root(g + groups, ln_var2, rstd2, ln_rstd2)

                def prep_split(g):
                    pool.wait_ge(z_rounded, g + groups + 1)
                    nc.gpsimd.tensor_tensor(of_group(zT_lo, g % 2), zT[:], of_group(zT_hi, g % 2).bitcast(F32),
                                            ALU.subtract).then_inc(z_split, 1)

                def prep_route(g):
                    pool.wait_ge(rt_step, g * RT + (groups * RT + RT_EXP))
                    nc.gpsimd.tensor_tensor(r_exp[:], euler[:], r_c[:], ALU.pow).then_inc(exp_ready, 1)

                def split_h(g, s):
                    n = g * STEPS + (s + base)
                    pool.wait_ge(hi_ready, n + 1)
                    nc.gpsimd.tensor_tensor(h_lo[:, s % LAG, :], h[:, s % LAG, :], h_hi[:, s % LAG, :].bitcast(F32),
                                            ALU.subtract).then_inc(lo_ready, 1)

                def window(g, k0, k1, last):
                    for k in range(k0, k1):
                        if k >= 1:
                            split_h(*group_step(g, k - 1))
                        if not last:
                            if k == AT_STATS:
                                prep_stats(g + 1)
                            if k == AT_NORM:
                                prep_norm(g + 1)
                            if k == AT_SPLIT:
                                prep_split(g + 1)
                            if k == AT_ROUTE:
                                prep_route(g + 1)
                    if last:
                        split_h(g, STEPS - 1)

                prep_stats(0)
                prep_norm(0)
                prep_split(0)
                prep_route(0)
                ffn_windows(pool, window)

            ffn(0)

            def attend(g0, events):
                for ev in events:
                    kind, use = ev[0], ev[-1]
                    if kind == "LN":
                        if ev[1]:
                            pool.wait_ge(q_ready, g0 * HI + HI)
                        inverse_root(g0 + (ev[1] + NG), ln_var, rstd, ln_rstd)
                    elif kind == "PROJ":
                        u = ev[1]
                        i = u % HI
                        pool.wait_ge(s_freed, g0 * RING + (RING0 + use + 1))
                        if u >= 1:
                            pool.wait_ge(q_ready, g0 * HI + u)
                        nc.gpsimd.tensor_tensor(q_stack[0:QROWS, i, :], q_fp[:, u % 2, :], one_of(QROWS), ALU.mult).then_inc(q_rounded, 1)
                        pool.wait_ge(q_rounded, g0 * HI + (u + 1))
                        nc.gpsimd.tensor_tensor(q_stack[64:96, i, :], q_fp[64:96, u % 2, :],
                                                q_stack[64:96, i, :].bitcast(F32), ALU.subtract).then_inc(q_ready, 1)
                    elif kind == "YT" and ev[2] == 1:
                        g = g0 + ev[1]
                        pool.wait_ge(s_freed, g0 * RING + (RING0 + use + 1))
                        nc.gpsimd.tensor_tensor(yT_hi, zT[:], one_of(P), ALU.mult).then_inc(y_rounded, 1)
                        pool.wait_ge(y_rounded, g + 1)
                        nc.gpsimd.tensor_tensor(yT_lo, zT[:], yT_hi.bitcast(F32), ALU.subtract).then_inc(y_split, 1)
                        nc.gpsimd.tensor_tensor(of_group(x, g), of_group(x, g), z[:].rearrange("p t f -> p (t f)"),
                                                ALU.add).then_inc(y_added, 1)

            pool.wait_ge(ones_set, 1)
            att_windows(pool, attend)
            pool.wait_ge(q_ready, NG * HI)
            ffn(1)


def kernel(L0_attn_queries, L0_attn_keys, L0_attn_values, L0_attn_Wq_w, L0_attn_Wq_b, L0_attn_Wk_w, L0_attn_Wk_b,
           L0_attn_Wv_w, L0_attn_Wv_b, L0_ffn_ln_scale, L0_ffn_ln_bias, L0_ffn_gate_w, L0_ffn_Wg, L0_ffn_Wu, L0_ffn_Wd,
           L0_ffn_sWg, L0_ffn_sWu, L0_ffn_sWd):
    import concourse.bacc as bacc
    from concourse.bass_utils import run_bass_kernel_spmd

    f32 = np.float32

    def arr(a):
        return np.ascontiguousarray(np.asarray(a))

    def stack_weights(w):
        w = arr(w).T.reshape(H, HJ, HI, DH).transpose(0, 2, 1, 3).reshape(H, HI, 1, HJ * DH)
        return np.ascontiguousarray(np.repeat(w, 3, axis=2).reshape(H, HI * QROWS))

    def stack_bias(b):
        b = arr(b).reshape(HJ, HI, DH).transpose(0, 2, 1).reshape(HJ * DH, HI)
        return np.ascontiguousarray(np.tile(b, (3, 1)))

    p = np.arange(P)
    copies = p[:, None] < QROWS
    head = np.where(copies, (p[:, None] % 32) // DH == np.arange(HJ), (p[:, None] - QROWS) % HJ == np.arange(HJ))
    head = head & (p[:, None] < QROWS + 2 * HJ)
    expert = (p[:, None] == np.arange(NE)) | (p[:, None] == 32 + np.arange(NE))
    lower = np.arange(NE)[None, :] < np.arange(NE)[:, None]
    arrays = {
        "x": arr(L0_attn_queries), "keysT": arr(arr(L0_attn_keys)[0].T), "valuesT": arr(arr(L0_attn_values)[0].T),
        "wq": stack_weights(L0_attn_Wq_w), "wk": stack_weights(L0_attn_Wk_w), "wvT": arr(arr(L0_attn_Wv_w).T),
        "bq": stack_bias(L0_attn_Wq_b), "bk": stack_bias(L0_attn_Wk_b),
        "bv": np.ascontiguousarray(np.tile(arr(L0_attn_Wv_b)[None, :], (P, 1))),
        "ln_scale": arr(L0_ffn_ln_scale).reshape(H, 1), "ln_bias": arr(L0_ffn_ln_bias).reshape(H, 1),
        "gate_t": arr(arr(L0_ffn_gate_w).T), "Wg": arr(L0_ffn_Wg), "Wu": arr(L0_ffn_Wu), "Wd": arr(L0_ffn_Wd),
        "sWg": arr(L0_ffn_sWg), "sWu": arr(L0_ffn_sWu), "sWd": arr(L0_ffn_sWd),
        "c_ident": np.eye(P, dtype=f32), "c_head": head.astype(f32), "c_expert": expert.astype(f32),
        "c_lower": np.ascontiguousarray(np.broadcast_to(lower.reshape(1, NE * NE), (P, NE * NE)).astype(f32)),
    }
    nc = bacc.Bacc("TRN2", target_bir_lowering=False, num_devices=1)
    d = {n: nc.dram_tensor(f"in_{n}", a.shape, mybir.dt.from_np(a.dtype), kind="ExternalInput").ap() for n, a in arrays.items()}
    d["out"] = nc.dram_tensor("out_x", (NB, S, H), F32, kind="ExternalOutput").ap()
    build(nc, d)
    r = run_bass_kernel_spmd(nc, [{f"in_{n}": a for n, a in arrays.items()}], core_ids=[0])
    return r.results[0]["out_x"]
```

```python
from contextlib import ExitStack

import numpy as np

import concourse.bass as bass
from concourse import mybir

F32 = mybir.dt.float32
F32R = mybir.dt.float32r
ALU = mybir.AluOpType
ACT = mybir.ActivationFunctionType
AX = mybir.AxisListType

P = 128
NB, S, H = 16, 256, 128
KEYS, NH, DH = 512, 16, 8
NE, TOPK, INTER = 8, 2, 256
LN_EPS, TOPK_EPS = 1e-5, 1e-5
GT = 4
GTOK = GT * P
NG = NB * S // GTOK
EXP = NE + 1
STEPS = 2 * EXP
KB = KEYS // P
HI, HJ = 4, 4
WCOLS = 2 * INTER + 2 * H
LAG = 3
PRE = 6
RAW = 3
QROWS = 96
LN_VAR = 7
RT, RT_SILU = 27, 7
RING_KINDS = ("S", "PROJ", "YT", "MT")
IN_C, IN_K = 7 * 16, 8 * 16
POOL_SETS = 8
PLACED = 16 * 8
RECIPS = 6


def build(nc, d):
    with ExitStack() as ctx:
        def sb(name, shape, dt=F32):
            return ctx.enter_context(nc.sbuf_tensor(name, shape, dt))

        def sem(name):
            return ctx.enter_context(nc.semaphore(name))

        psum = ctx.enter_context(nc.psum_tensor("psum", [P, 8, 512], F32))

        x = sb("x", [P, NG, GTOK])
        ident = sb("ident", [P, P])
        w_hi = sb("w_hi", [P, EXP, WCOLS], F32R)
        w_lo = sb("w_lo", [P, EXP, WCOLS], F32R)
        k_stack = sb("k_stack", [P, HI, HJ, KEYS], F32R)
        v_pad = sb("v_pad", [P, KB, HI, HJ, 32])
        minus_half = sb("minus_half", [P, GT])
        mean = sb("mean", [P, GT])
        mean2 = sb("mean2", [P, GT])
        stats = sb("stats", [P, GT, 6])
        ln_tmp = sb("ln_tmp", [P, 5, GT])
        var_eps = sb("var_eps", [P, GT])
        rstd = sb("rstd", [P, GT])
        rstd2 = sb("rstd2", [P, GT])
        z = sb("z", [P, GT, H])
        zT = sb("zT", [P, GTOK])
        staging = sb("staging", [P, RAW * WCOLS])
        w_raw = staging[:].rearrange("p (r c) -> p r c", r=RAW)
        zT_hi = sb("zT_hi", [P, 2, GTOK], F32R)
        zT_lo = sb("zT_lo", [P, 2, GTOK], F32R)
        gate_t = sb("gate_t", [P, NE])
        ln_scale = sb("ln_scale", [P, 1])
        ln_bias = sb("ln_bias", [P, 1])
        gate_s = sb("gate_s", [P, 2, NE])
        gate_sum = sb("gate_sum", [P, 2, NE])
        ones = sb("ones", [P, P])
        lower = sb("lower", [P, NE, NE])
        expert_ind = sb("expert_ind", [P, NE])
        expert_sel = sb("expert_sel", [P, NE, P], F32R)
        r_a = sb("r_a", [P, GT, NE])
        r_b = sb("r_b", [P, GT, NE])
        r_c = sb("r_c", [P, GT, NE])
        r_silu = sb("r_silu", [P, GT, NE])
        r_1 = sb("r_1", [P, GT])
        r_2 = sb("r_2", [P, GT])
        r_3 = sb("r_3", [P, GT])
        r_gt = sb("r_gt", [P, GT, NE, NE])
        r_eq = sb("r_eq", [P, GT, NE, NE])
        route = sb("route", [P, GT, P], F32R)
        route_T = sb("route_T", [P, 2, GTOK], F32R)
        silu = sb("silu", [P, 2, GTOK])
        act_up = sb("act_up", [P, GTOK])
        h = sb("h", [P, LAG, GTOK])
        h_hi = sb("h_hi", [P, LAG, GTOK], F32R)
        h_lo = sb("h_lo", [P, LAG, GTOK], F32R)
        out_T = sb("out_T", [P, GTOK])
        wq_hi = sb("wq_hi", [P, HI, QROWS], F32R)
        wq_lo = sb("wq_lo", [P, HI, QROWS], F32R)
        wk = sb("wk", [P, HI, QROWS])
        wvT = sb("wvT", [P, H])
        bq = sb("bq", [QROWS, HI])
        bk = sb("bk", [QROWS, HI])
        bv = sb("bv", [P, H])
        head_ind = sb("head_ind", [P, HJ])
        q_stack = sb("q_stack", [P, HI, GTOK], F32R)
        k_parts = q_stack
        yT_hi, yT_lo = zT_hi[:, 0, :], zT_lo[:, 0, :]
        q_fp = sb("q_fp", [32, 2, GTOK])
        neg_max = sb("neg_max", [P, 2, GT, HJ])
        max_stage = sb("max_stage", [P, GT, P], F32R)
        probs = sb("probs", [P, 2, HJ, GTOK])
        k_fp, keysT, valuesT = probs[0:QROWS, 0, :, :], probs[:, 1, 0, :], probs[:, 1, 1, :]
        v_fp = probs[:, 1, 2, :].rearrange("p (k c) -> p k c", k=KB)
        wq_raw = probs[:, 1, 3, 0:HI * QROWS].rearrange("p (i c) -> p i c", i=HI)
        acc_a, acc_b, num, den = (staging[:, n * GTOK:(n + 1) * GTOK] for n in range(4))
        rden = out_T[:]

        in_c, in_k = sem("in_consts"), sem("in_attention")
        in_x = [sem(f"in_x{g}") for g in range(NG)]
        in_w = [sem(f"in_w{r}") for r in range(RAW)]
        gates_scaled, ones_set, pool_set, sel_set = sem("gates_scaled"), sem("ones_set"), sem("pool_set"), sem("sel_set")
        w_rounded, w_split = sem("w_rounded"), sem("w_split")
        k_projected, v_projected, gates_summed = sem("k_projected"), sem("v_projected"), sem("gates_summed")
        k_ready, k_rounded, k_split, k_stacked = sem("k_ready"), sem("k_rounded"), sem("k_split"), sem("k_stacked")
        wq_rounded, wq_split, v_ready, v_padded, sums_read = (sem("wq_rounded"), sem("wq_split"), sem("v_ready"),
                                                              sem("v_padded"), sem("sums_read"))
        ln_stat, ln_var, ln_rstd, ln_done = sem("ln_stat"), sem("ln_var"), sem("ln_rstd"), sem("ln_done")
        ln_stat2, ln_var2, ln_rstd2 = sem("ln_stat2"), sem("ln_var2"), sem("ln_rstd2")
        z_turned, z_copied, z_rounded, z_split = sem("z_turned"), sem("z_copied"), sem("z_rounded"), sem("z_split")
        logits_ready, rt_step, rt_silu = sem("logits_ready"), sem("rt_step"), sem("rt_silu")
        route_turned, route_copied = sem("route_turned"), sem("route_copied")
        gate_ready, up_ready, bc_ready, down_done = sem("gate_ready"), sem("up_ready"), sem("bc_ready"), sem("down_done")
        silu_ready, up_used, h_ready = sem("silu_ready"), sem("up_used"), sem("h_ready")
        hi_ready, lo_ready = sem("hi_ready"), sem("lo_ready")
        out_copied, out_turned, x_updated = sem("out_copied"), sem("out_turned"), sem("x_updated")
        s_filled, s_freed = sem("s_filled"), sem("s_freed")
        m_filled, m_freed = sem("m_filled"), sem("m_freed")
        q_rounded, q_ready = sem("q_rounded"), sem("q_ready")
        y_rounded, y_split, y_added = sem("y_rounded"), sem("y_split"), sem("y_added")
        max_hi, max_lo = sem("max_hi"), sem("max_lo")
        av_done, acc_copied = sem("av_done"), sem("acc_copied")
        num_placed, den_placed = sem("num_placed"), sem("den_placed")
        recip_done, att_done, x_attended = sem("recip_done"), sem("att_done"), sem("x_attended")
        stored = sem("stored")

        G_BANK, U_BANK, BC_BANK, OUT_BANK, Z_BANK, R_BANK = (0, 1), (2, 3), 4, 5, 6, 7
        S_BANK, A_BANK, B_BANK, M_BANK = (0, 2), 4, 5, (6, 7)
        KP_BANK, VP_BANK, GS_BANK = (0, 1, 2, 3), 4, 5

        def bank(b, rows=P):
            return psum[0:rows, b, :]

        def of_group(buf, g):
            return buf[:, bass.ds(g, 1), :].rearrange("p a n -> p (a n)")

        block = ctx.enter_context(nc.Block())

        def ffn_windows(eng, window):
            window(0, 0, PRE, False)
            with eng.Fori(0, NG - 1) as g:
                window(g, PRE, PRE + STEPS, False)
            window(NG - 1, PRE, STEPS, True)

        def group_step(g, k):
            return (g + 1, k - STEPS) if k >= STEPS else (g, k)

        AT_STATS, AT_NORM, AT_STATS2, AT_TURN, AT_COPY, AT_SPLIT, AT_LOGITS = 6, 7, 8, 8, 9, 10, 10
        AT_ROUTE = {11: 0, 12: 1, 14: 2, 15: 3, 16: 4, 17: 5}
        AT_ROUTE_SILU, AT_ROUTE_TURN, AT_ROUTE_COPY = 13, 18, 19
        AT_OUT, AT_OUT_TURN, AT_UPDATE = STEPS + LAG, STEPS + LAG + 1, STEPS + LAG + 2

        AV_LAG = 2
        AT_RECIP, STEP0 = 3, 6

        def att_events(k, last):
            dg, r = divmod(k, HI * KB)
            i, kb = divmod(r, KB)
            u = HI * dg + i
            ahead = u + (2 if kb == KB - 1 else 1)
            m = [] if last and ahead >= HI else [("M", ahead, (kb + 1) % GT, j) for j in range(HJ)]
            recip = [("RECIP", dg - 1, 2 * (r - AT_RECIP) + n) for n in range(2) if 0 <= 2 * (r - AT_RECIP) < RECIPS]
            out = m[:2] + recip[:1]
            if not last:
                out += {6: [("LNS", dg + 1)], 7: [("LNN", dg + 1)], 8: [("YT", dg + 1, 0)], 9: [("YT", dg + 1, 1)]}.get(r, [])
            if kb == (2 if i == HI - 2 else 0) and not (last and u + 2 >= HI):
                out += [("PROJ", u + 2)]
            if kb == KB - 1 and not (last and u + 1 >= HI):
                out += [("MT", u + 1)]
            out += [("AV", k - AV_LAG)]
            if r % (2 * KB) == AV_LAG - 1:
                out += [("EVAC", 2 * dg + i // 2 - 1)]
            out += m[2:] + recip[1:] + [("S", u, kb, 0), ("S", u, kb, 1)]
            if r == STEP0 - 1:
                out += [("POST", dg - 1)]
            return out

        def number(events, start):
            out = []
            for ev in events:
                out.append((*ev, start) if ev[0] in RING_KINDS else ev)
                start += ev[0] in RING_KINDS
            return out

        EARLY_USES = 4
        first_maxima = [("M", 0, qt, j) for qt in range(GT) for j in range(HJ)]
        beside = {6: [("LNS", 0), ("LNN", 0)], 8: [("YT", 0, 0), ("YT", 0, 1)], 10: [("PROJ", 0)], 12: [("PROJ", 1)]}
        beside.update({k: first_maxima[2 * (k - 13):2 * (k - 12)] for k in range(13, STEPS)})
        opening = first_maxima[2 * (STEPS - 13):] + [("MT", 0)] + [("M", 1, 0, j) for j in range(HJ)]
        opening += [e for k in range(STEP0) for e in att_events(k, False)
                    if not (e[0] in ("AV", "EVAC", "RECIP", "POST") and e[1] < 0)]
        RING0 = EARLY_USES + sum(e[0] in RING_KINDS for e in opening)
        opening = number(opening, EARLY_USES - RING0)
        uses = -RING0
        for k, events in beside.items():
            beside[k] = number(events, uses)
            uses += sum(e[0] in RING_KINDS for e in events)
        middle = number([e for k in range(STEP0, STEP0 + HI * KB) for e in att_events(k, False)], 0)
        RING = sum(e[0] in RING_KINDS for e in middle)
        final = [e for k in range(STEP0, HI * KB) for e in att_events(k, True)]
        for k, names in {11: ["stats"], 12: ["norm"], 13: ["stats2", "turn"], 14: ["copy", "split", "logits"], 15: ["route"]}.items():
            at = final.index(("AV", k - AV_LAG)) + 1
            final[at:at] = [("NEXT", name) for name in names]
        final = number(final + [("AV", HI * KB - n) for n in range(AV_LAG, 0, -1)] + [("EVAC", 1)], 0)
        RING_END = sum(e[0] in RING_KINDS for e in final)
        assert RING % 2 == 0

        def ring_uses(events):
            mt, sc = {}, {}
            for ev in opening + (events if events is not opening else []):
                if ev[0] == "MT":
                    mt[ev[1]] = ev[-1]
                if ev[0] == "S" and ev[3] == 1:
                    sc[ev[1] * KB + ev[2]] = ev[-1]
            return mt, sc

        def ring_bank(use):
            if use < EARLY_USES - RING0:
                return (Z_BANK, R_BANK)[(RING0 + use) % 2]
            return S_BANK[(RING0 + use) % 2]

        def att_windows(eng, window):
            window(0, opening)
            with eng.Fori(0, NG - 1) as g:
                window(g, middle)
            window(NG - 1, final)

        @block.sync
        def _(sp):
            def load_x(g):
                sp.dma_start(x[:, g, :].rearrange("p (b n) -> p b n", b=2),
                             d["x"][2 * g:2 * g + 2].rearrange("b (p t) f -> p b (t f)", t=2)).then_inc(in_x[g], 16)

            def load_expert(e):
                if e >= RAW:
                    sp.wait_ge(w_split, e - RAW + 1)
                wg, wu, wd = (d["sWg"], d["sWu"], d["sWd"]) if e == 0 else (d["Wg"][e - 1], d["Wu"][e - 1], d["Wd"][e - 1])
                r = e % RAW
                sp.dma_start(w_raw[:, r, 0:INTER], wg).then_inc(in_w[r], 16)
                sp.dma_start(w_raw[:, r, INTER:2 * INTER], wu).then_inc(in_w[r], 16)
                sp.dma_start(w_raw[:, r, 2 * INTER:].rearrange("p (i n) -> p i n", i=2),
                             wd.rearrange("(i p) n -> p i n", i=2)).then_inc(in_w[r], 16)

            load_x(0)
            for to, of in ((ident[:], "c_ident"), (expert_ind[:], "c_expert"), (lower[:].rearrange("p e f -> p (e f)"), "c_lower"),
                           (head_ind[:], "c_head"), (gate_t[:], "gate_t"), (ln_scale[:], "ln_scale"), (ln_bias[:], "ln_bias")):
                sp.dma_start(to, d[of]).then_inc(in_c, 16)
            for e in range(EXP):
                load_expert(e)
                if e == RAW - 1:
                    load_x(1)
            for g in range(2, NG):
                load_x(g)

            half = 2 * DH
            def place(g):
                sp.wait_ge(x_attended, g)
                for n, of in ((0, acc_a), (1, acc_b)):
                    sp.wait_ge(acc_copied, 2 * g + (n + 1))
                    for to, f0, done in ((den, half, den_placed), (num, 0, num_placed)):
                        for j in range(HJ):
                            sp.dma_start(to[32 * j + n * half:32 * j + (n + 1) * half, :],
                                         of[32 * j + f0:32 * j + f0 + half, :]).then_inc(done, 16)

            with sp.Fori(0, NG) as g:
                place(g)
            with sp.Fori(0, NG) as g:
                sp.wait_ge(x_updated, g + (NG + 1))
                for b in range(2):
                    sp.dma_start(d["out"][bass.ds(2 * g + b, 1)].rearrange("b (p t) f -> (b p) (t f)", t=2),
                                 x[:, bass.ds(g, 1), b * S:(b + 1) * S].rearrange("p a n -> p (a n)")).then_inc(stored, 16)
            sp.wait_ge(stored, 16 * NB)

        @block.tensor
        def _(pe):
            mm = nc.tensor.matmul

            def three(out, w, wl, m, ml, start, stop):
                mm(out, w, m, start=start, stop=False)
                mm(out, w, ml, start=False, stop=False)
                return mm(out, wl, m, start=False, stop=stop)

            def turn(out, in_):
                return nc.tensor.transpose(out, in_, ident[:])

            pe.wait_ge(in_c, IN_C)
            pe.wait_ge(ones_set, 1)
            pe.wait_ge(gates_scaled, 2)
            mm(psum[:, GS_BANK, 0:2 * NE], ones[:], gate_s[:].rearrange("p a e -> p (a e)"),
               start=True, stop=True).then_inc(gates_summed, 1)

            def ffn(ph):
                base, groups = ph * NG * STEPS, ph * NG

                def prep_z(g):
                    pe.wait_ge(ln_done, g + 2 * groups + 1)
                    if not (isinstance(g, int) and g == 0):
                        pe.wait_ge(x_updated, g + groups - 1)
                    for t in range(GT):
                        last = turn(psum[:, Z_BANK, t * P:(t + 1) * P], z[:, t, :])
                    last.then_inc(z_turned, 1)

                def prep_logits(g):
                    pe.wait_ge(z_copied, g + groups + 1)
                    pe.wait_ge(route_copied, g + groups)
                    for t in range(GT):
                        last = mm(psum[:, R_BANK, t * NE:(t + 1) * NE], zT[:, t * P:(t + 1) * P], gate_s[:, 0, :],
                                  start=True, stop=True)
                    last.then_inc(logits_ready, 1)

                def turn_route(g):
                    pe.wait_ge(rt_step, g * RT + (groups * RT + RT))
                    for t in range(GT):
                        last = turn(psum[:, R_BANK, t * P:(t + 1) * P], route[:, t, :].bitcast(F32))
                    last.then_inc(route_turned, 1)

                def gate_up(g, s):
                    n = g * STEPS + (s + base)
                    e, i = divmod(s, 2)
                    opens = ph == 0 and isinstance(g, int) and g == 0 and s < 2
                    zh, zl = of_group(zT_hi, g % 2), of_group(zT_lo, g % 2)
                    if s == 0:
                        pe.wait_ge(z_split, g + groups + 1)
                    if ph == 0 and isinstance(g, int) and g == 0:
                        pe.wait_ge(w_split, e + 1)
                    if not opens:
                        pe.wait_ge(silu_ready, n - 1)
                    c = i * P
                    three(bank(G_BANK[s % 2]), w_hi[:, e, c:c + P], w_lo[:, e, c:c + P], zh, zl,
                          True, True).then_inc(gate_ready, 1)
                    if not opens:
                        pe.wait_ge(up_used, n - 1)
                    c = INTER + i * P
                    three(bank(U_BANK[s % 2]), w_hi[:, e, c:c + P], w_lo[:, e, c:c + P], zh, zl,
                          True, True).then_inc(up_ready, 1)

                def down(g, s):
                    n = g * STEPS + (s + base)
                    e, i = divmod(s, 2)
                    pe.wait_ge(lo_ready, n + 1)
                    if s == 0:
                        pe.wait_ge(out_copied, g + groups)
                    if ph == 1 and isinstance(g, int) and g == 0 and s == 0:
                        pe.wait_ge(acc_copied, 2 * NG)
                    c = 2 * INTER + i * H
                    three(bank(OUT_BANK), w_hi[:, e, c:c + H], w_lo[:, e, c:c + H], h_hi[:, s % LAG, :],
                          h_lo[:, s % LAG, :], s == 0, s == STEPS - 1).then_inc(down_done, 1)

                def broadcast(g, s):
                    e = s // 2 - 1
                    if ph == 0 and e == 0:
                        pe.wait_ge(sel_set, 1)
                    if e == 0:
                        pe.wait_ge(route_copied, g + groups + 1)
                    pe.wait_ge(h_ready, g * (2 * NE) + (groups * 2 * NE + 2 * e))
                    mm(bank(BC_BANK), expert_sel[:, e, :], of_group(route_T, g % 2),
                       start=True, stop=True).then_inc(bc_ready, 1)

                def finish(g, last_group):
                    pe.wait_ge(out_copied, g + groups + 1)
                    if last_group:
                        pe.wait_ge(h_ready, (groups + NG) * 2 * NE)
                    else:
                        pe.wait_ge(z_copied, g + groups + 2)
                    for t in range(GT):
                        last = turn(psum[:, BC_BANK if last_group else Z_BANK, t * P:(t + 1) * P], out_T[:, t * P:(t + 1) * P])
                    last.then_inc(out_turned, 1)

                def window(g, k0, k1, last):
                    for k in range(k0, k1):
                        gg, s = group_step(g, k)
                        if ph == 0 and k == PRE and not last:
                            pe.wait_ge(w_split, EXP)
                        gate_up(gg, s)
                        if k >= LAG:
                            down(*group_step(g, k - LAG))
                        if k == 2:
                            turn_route(g)
                        if s >= 2 and s % 2 == 0:
                            broadcast(gg, s)
                        if not last:
                            if k == AT_TURN:
                                prep_z(g + 1)
                            if k == AT_LOGITS:
                                prep_logits(g + 1)
                            if k == AT_ROUTE_TURN:
                                turn_route(g + 1)
                            if k == AT_OUT_TURN:
                                finish(g, False)
                        if last and ph == 0:
                            attend(0, beside.get(k, []))
                    if last:
                        for k in range(STEPS - LAG, STEPS):
                            down(g, k)
                        finish(g, True)

                def run():
                    if ph == 1:
                        pe.wait_ge(s_freed, RING * (NG - 1) + RING0 + RING_END)
                    ffn_windows(pe, window)

                return {"turn": lambda: prep_z(0), "logits": lambda: prep_logits(0), "run": run}

            first, second = ffn(0), ffn(1)
            def attend(g0, events):
                mt_use, s_use = ring_uses(events)

                def claim(use):
                    if use >= 2 - RING0:
                        pe.wait_ge(s_freed, g0 * RING + (RING0 + use - 1))
                    return ring_bank(use)

                for ev in events:
                    kind, use = ev[0], ev[-1]
                    if kind == "NEXT" and ev[1] == "turn":
                        pe.wait_ge(m_freed, 64 * NG)
                    if kind == "NEXT" and ev[1] in second:
                        second[ev[1]]()
                    if kind == "S":
                        _, u, kb, jp, _ = ev
                        i = u % HI
                        if kb == 0 and jp == 0:
                            pe.wait_ge(s_freed, g0 * RING + (RING0 + mt_use[u] + 1))
                        b = claim(use)
                        for j in (2 * jp, 2 * jp + 1):
                            last = mm(bank(b + j % 2), k_stack[:, i, j, kb * P:(kb + 1) * P], q_stack[:, i, :],
                                      start=True, stop=True)
                        last.then_inc(s_filled, 1)
                    elif kind == "M":
                        _, u, qt, j = ev
                        i = u % HI
                        if qt == 0 and j == 0:
                            pe.wait_ge(q_ready, g0 * HI + (u + 1))
                        r = 16 * u + 4 * qt + j
                        if r == 0:
                            pe.wait_ge(k_stacked, HJ)
                            pe.wait_ge(s_freed, EARLY_USES)
                        if r >= 2:
                            pe.wait_ge(m_freed, g0 * 64 + (r - 1))
                        mm(bank(M_BANK[j % 2]), q_stack[0:QROWS, i, qt * P:(qt + 1) * P], k_stack[0:QROWS, i, j, :],
                           start=True, stop=True).then_inc(m_filled, 1)
                    elif kind == "PROJ":
                        i = ev[1] % HI
                        if i == 0:
                            pe.wait_ge(y_split, g0 * 2 + 2 * (ev[1] // HI + 1))
                        if use == 2 - RING0:
                            pe.wait_ge(wq_split, 1)
                        three(bank(claim(use), QROWS), wq_hi[:, i, :], wq_lo[:, i, :], yT_hi, yT_lo,
                              True, True).then_inc(s_filled, 1)
                    elif kind == "YT":
                        _, dg, half, _ = ev
                        pe.wait_ge(ln_done, g0 + (dg + NG + 1))
                        b = claim(use)
                        for t in range(2):
                            last = turn(psum[:, b, t * P:(t + 1) * P], z[:, 2 * half + t, :])
                        last.then_inc(s_filled, 1)
                    elif kind == "MT":
                        pe.wait_ge(max_lo, g0 * HI + (ev[1] + 1))
                        if use == EARLY_USES - RING0:
                            pe.wait_ge(silu_ready, NG * STEPS)
                            pe.wait_ge(up_used, NG * STEPS)
                        b = claim(use)
                        for t in range(GT):
                            last = turn(psum[:, b, t * P:(t + 1) * P], max_stage[:, t, :].bitcast(F32))
                        last.then_inc(s_filled, 1)
                    elif kind == "AV":
                        k = ev[1]
                        dg, r = divmod(k, HI * KB)
                        i, kb = divmod(r, KB)
                        pe.wait_ge(s_freed, g0 * RING + (RING0 + s_use[k] + 1))
                        if isinstance(g0, int) and g0 == 0 and k == 0:
                            pe.wait_ge(x_updated, NG)
                            pe.wait_ge(v_padded, HI)
                        if kb == 0 and i % 2 == 0 and 2 * dg + i // 2 - 1 >= 0:
                            pe.wait_ge(acc_copied, g0 * 2 + (2 * dg + i // 2 - 1))
                        for j in range(HJ):
                            last = mm(psum[32 * j:32 * j + 32, A_BANK if i < 2 else B_BANK, :],
                                      v_pad[:, kb, i, j, :], probs[:, kb % 2, j, :],
                                      start=(i % 2 == 0 and kb == 0), stop=(i % 2 == 1 and kb == KB - 1))
                        last.then_inc(av_done, 1)

            first["turn"]()
            first["logits"]()
            pe.wait_ge(in_k, IN_K)
            for i in range(HI):
                mm(bank(KP_BANK[i], QROWS), wk[:, i, :], keysT, start=True, stop=True).then_inc(k_projected, 1)
            for kb in range(KB):
                last = mm(psum[:, VP_BANK, kb * H:(kb + 1) * H], valuesT[:, kb * P:(kb + 1) * P], wvT[:],
                          start=True, stop=True)
            last.then_inc(v_projected, 1)
            pe.wait_ge(k_ready, 2 * HI)
            pe.wait_ge(v_ready, 1)
            pe.wait_ge(sums_read, 1)
            pe.wait_ge(sel_set, 1)
            first["run"]()
            att_windows(pe, attend)
            second["run"]()

        @block.scalar
        def _(act):
            for to, of in ((wk[:].rearrange("p i c -> p (i c)"), "wk"), (keysT, "keysT"), (wvT[:], "wvT"), (valuesT, "valuesT"),
                           (wq_raw.rearrange("p i c -> p (i c)"), "wq"), (bq[:], "bq"), (bk[:], "bk"), (bv[:], "bv")):
                act.dma_start(to, d[of]).then_inc(in_k, 16)
            def round_expert(e):
                act.wait_ge(in_w[e % RAW], 48 * (e // RAW + 1))
                nc.scalar.copy(w_hi[:, e, :], w_raw[:, e % RAW, :]).then_inc(w_rounded, 1)

            def ffn(ph):
                base, groups = ph * NG * STEPS, ph * NG

                def copy_z(g):
                    act.wait_ge(z_turned, g + groups + 1)
                    act.wait_ge(z_split, g + groups)
                    act.wait_ge(logits_ready, g + groups)
                    if ph == 1:
                        act.wait_ge(y_split, 2 * NG)
                    nc.scalar.copy(zT[:], bank(Z_BANK)).then_inc(z_copied, 1)

                def route_silu(g):
                    act.wait_ge(rt_step, g * RT + (groups * RT + RT_SILU))
                    nc.scalar.activation(r_silu[:], r_c[:], ACT.Silu).then_inc(rt_silu, 1)

                def copy_route(g):
                    act.wait_ge(route_turned, g + groups + 1)
                    nc.scalar.copy(of_group(route_T, g % 2), bank(R_BANK)).then_inc(route_copied, 1)

                def copy_out(g):
                    act.wait_ge(down_done, g * STEPS + (base + STEPS))
                    act.wait_ge(out_turned, g + groups)
                    nc.scalar.copy(out_T[:], bank(OUT_BANK)).then_inc(out_copied, 1)

                def gates(g, s):
                    n = g * STEPS + (s + base)
                    act.wait_ge(gate_ready, n + 1)
                    if not (ph == 0 and isinstance(g, int) and g == 0 and s < 2):
                        act.wait_ge(up_used, n - 1)
                    nc.scalar.activation(silu[:, s % 2, :], bank(G_BANK[s % 2]), ACT.Silu).then_inc(silu_ready, 1)

                def round_h(g, s):
                    n = g * STEPS + (s + base)
                    if s < 2:
                        act.wait_ge(up_used, n + 1)
                    else:
                        act.wait_ge(h_ready, g * (2 * NE) + (groups * 2 * NE + s - 1))
                    if not (ph == 0 and isinstance(g, int) and g == 0 and s < LAG):
                        act.wait_ge(down_done, n - (LAG - 1))
                    nc.scalar.copy(h_hi[:, s % LAG, :], h[:, s % LAG, :]).then_inc(hi_ready, 1)

                def window(g, k0, k1, last):
                    for k in range(k0, k1):
                        if last and ph == 0:
                            attend(0, beside.get(k - 1, []))
                            if 7 <= k < 7 + HJ:
                                j = k - 7
                                act.wait_ge(k_split, HI + 1)
                                nc.scalar.activation(k_stack[:, :, j, :], k_parts[:].bitcast(F32), ACT.Copy,
                                                     scale=head_ind[:, j:j + 1]).then_inc(k_stacked, 1)
                        if k == AT_OUT:
                            copy_out(g)
                        if not last and k == AT_ROUTE_COPY:
                            copy_route(g + 1)
                        gates(*group_step(g, k))
                        if k == 0:
                            route_silu(g)
                        if k >= 1:
                            round_h(*group_step(g, k - 1))
                        if k == 2:
                            copy_route(g)
                        if ph == 0 and k < PRE:
                            round_expert(RAW + k)
                        if ph == 0 and k == PRE - 1:
                            act.wait_ge(v_ready, 1)
                            act.wait_ge(pool_set, POOL_SETS)
                            v_heads = v_fp.rearrange("p k (j i c) -> p k i j c", i=HI, j=HJ)
                            for i in range(HI):
                                c = DH * (i % 2)
                                nc.scalar.activation(v_pad[:, :, i, :, c:c + DH], v_heads[:, :, i, :, :],
                                                     ACT.Relu).then_inc(v_padded, 1)
                        if not last:
                            if k == AT_COPY:
                                copy_z(g + 1)
                            if k == AT_ROUTE_SILU:
                                route_silu(g + 1)
                    if last:
                        round_h(g, STEPS - 1)
                        copy_out(g)
                        if ph == 0:
                            attend(0, beside.get(STEPS - 1, []))

                return {"copy": lambda: copy_z(0), "run": lambda: ffn_windows(act, window)}

            first, second = ffn(0), ffn(1)

            def attend(g0, events):
                for ev in events:
                    kind, use = ev[0], ev[-1]
                    if kind == "NEXT" and ev[1] in second:
                        second[ev[1]]()
                    if kind in RING_KINDS:
                        act.wait_ge(s_filled, g0 * RING + (RING0 + use + 1))
                        b = ring_bank(use)
                    if kind == "S":
                        _, u, kb, jp, _ = ev
                        k = u * KB + kb
                        if k >= 2 and jp == 0:
                            act.wait_ge(av_done, g0 * 16 + (k - 1))
                        nc.scalar.activation(probs[:, kb % 2, 2 * jp:2 * jp + 2, :], psum[:, b:b + 2, :], ACT.Exp,
                                             scale=float(DH) ** -0.5).then_inc(s_freed, 1)
                    elif kind == "PROJ":
                        u = ev[1]
                        if u >= 2:
                            act.wait_ge(q_ready, g0 * HI + (u - 1))
                        if use == 2 - RING0:
                            act.wait_ge(k_stacked, HJ)
                        nc.scalar.activation(q_stack[0:QROWS, u % HI, :], bank(b, QROWS), ACT.Relu,
                                             bias=bq[:, u % HI:u % HI + 1]).then_inc(q_rounded, 1)
                        nc.scalar.activation(q_fp[:, u % 2, :], psum[0:32, b, :], ACT.Relu,
                                             bias=bq[0:32, u % HI:u % HI + 1]).then_inc(s_freed, 1)
                    elif kind == "YT":
                        _, dg, half, _ = ev
                        act.wait_ge(y_split, g0 * 2 + 2 * dg)
                        cols = slice(2 * half * P, 2 * (half + 1) * P)
                        nc.scalar.copy(yT_hi[:, cols], psum[:, b, 0:2 * P]).then_inc(y_rounded, 1)
                        nc.scalar.copy(zT[:, cols], psum[:, b, 0:2 * P]).then_inc(s_freed, 1)
                    elif kind == "MT":
                        nc.scalar.copy(q_stack[QROWS:P, ev[1] % HI, :], psum[QROWS:P, b, :]).then_inc(s_freed, 1)
                    elif kind == "EVAC":
                        n = ev[1]
                        act.wait_ge(av_done, g0 * 16 + 8 * (n + 1))
                        act.wait_ge(num_placed, g0 * PLACED + PLACED * (n // 2))
                        act.wait_ge(den_placed, g0 * PLACED + PLACED * (n // 2))
                        nc.scalar.copy(acc_b if n % 2 else acc_a, bank(B_BANK if n % 2 else A_BANK)).then_inc(acc_copied, 1)

            round_expert(0)
            first["copy"]()
            for e in range(1, RAW):
                round_expert(e)
            act.wait_ge(in_k, IN_K)
            for i in range(HI):
                act.wait_ge(k_projected, i + 1)
                nc.scalar.activation(k_fp[:, i, :], bank(KP_BANK[i], QROWS), ACT.Relu, bias=bk[:, i:i + 1]).then_inc(k_ready, 1)
                nc.scalar.activation(k_parts[0:QROWS, i, :], bank(KP_BANK[i], QROWS), ACT.Relu, bias=bk[:, i:i + 1]).then_inc(k_ready, 1)
            first["run"]()
            att_windows(act, attend)
            second["run"]()

        @block.vector
        def _(dve):
            tt, ts = nc.vector.tensor_tensor, nc.vector.tensor_scalar
            stt, cp = nc.vector.scalar_tensor_tensor, nc.vector.tensor_copy

            def spread(v, n):
                return v.unsqueeze(2).broadcast_to([P, GT, n])

            nc.vector.memset(ones[:], 1.0).then_inc(ones_set, 1)
            dve.wait_ge(in_c, IN_C)
            ts(gate_s[:, 0, :], gate_t[:], ln_scale[:], None, ALU.mult).then_inc(gates_scaled, 1)
            ts(gate_s[:, 1, :], gate_t[:], ln_bias[:], None, ALU.mult).then_inc(gates_scaled, 1)
            def moments(n, rows, stat_sem, var_sem, mean_out):
                for t in range(GT):
                    nc.vector.bn_stats(stats[:, t, :], rows[:, t * H:(t + 1) * H]).then_inc(stat_sem, 1)
                dve.wait_ge(stat_sem, n * GT + GT)
                mean_e, mean_o, m2_e, m2_o = (stats[:, :, c] for c in (1, 4, 2, 5))
                total, apart, apart2, m2, var = (ln_tmp[:, c, :] for c in range(5))
                tt(total, mean_e, mean_o, ALU.add).then_inc(var_sem, 1)
                tt(apart, mean_e, mean_o, ALU.subtract).then_inc(var_sem, 1)
                tt(m2, m2_e, m2_o, ALU.add).then_inc(var_sem, 1)
                dve.wait_ge(var_sem, n * LN_VAR + 3)
                ts(mean_out[:], total, 0.5, None, ALU.mult).then_inc(var_sem, 1)
                stt(out=apart2, in0=apart, scalar=0.25, in1=apart, op0=ALU.mult, op1=ALU.mult).then_inc(var_sem, 1)
                ts(var, m2, 1.0 / H, LN_EPS, ALU.mult, ALU.add).then_inc(var_sem, 1)
                dve.wait_ge(var_sem, n * LN_VAR + 6)
                tt(var_eps[:], var, apart2, ALU.add).then_inc(var_sem, 1)

            def norm_stats(n, g):
                moments(n, of_group(x, g), ln_stat, ln_var, mean)

            def norm(n, g):
                dve.wait_ge(ln_rstd, n + 1)
                for t in range(GT):
                    last = ts(z[:, t, :], of_group(x, g)[:, t * H:(t + 1) * H], mean[:, t:t + 1], rstd[:, t:t + 1],
                              ALU.subtract, ALU.mult)
                last.then_inc(ln_done, 1)

            def ffn(ph):
                base, groups = ph * NG * STEPS, ph * NG

                def prep_stats(g):
                    if ph == 0 and isinstance(g, int):
                        dve.wait_ge(in_x[g], 16)
                    if ph == 1:
                        dve.wait_ge(x_attended, g + 1)
                    norm_stats(g + 2 * groups, g)

                def prep_norm(g):
                    dve.wait_ge(z_turned, g + groups)
                    if ph == 1:
                        dve.wait_ge(y_added, NG)
                    norm(g + 2 * groups, g)

                def prep_stats2(g):
                    dve.wait_ge(ln_done, g + (2 * groups + 1))
                    moments(g + groups, z[:].rearrange("p t f -> p (t f)"), ln_stat2, ln_var2, mean2)

                def prep_round(g):
                    dve.wait_ge(z_copied, g + groups + 1)
                    cp(of_group(zT_hi, g % 2), zT[:]).then_inc(z_rounded, 1)

                def prep_route(g, part):
                    n = g + groups

                    def done(ins):
                        ins.then_inc(rt_step, 1)

                    def after(step):
                        dve.wait_ge(rt_step, n * RT + step)

                    if part == 0:
                        logits = psum[:, R_BANK, 0:GT * NE].rearrange("p (t e) -> p t e", t=GT)
                        dve.wait_ge(logits_ready, n + 1)
                        dve.wait_ge(ln_rstd2, n + 1)
                        done(tt(r_a[:], gate_sum[:, 0, :].unsqueeze(1).broadcast_to([P, GT, NE]), spread(mean2[:], NE), ALU.mult))
                        after(1)
                        done(tt(r_b[:], logits, r_a[:], ALU.subtract))
                        after(2)
                        done(tt(r_a[:], r_b[:], spread(rstd2[:], NE), ALU.mult))
                        after(3)
                        done(tt(r_b[:], r_a[:], gate_sum[:, 1, :].unsqueeze(1).broadcast_to([P, GT, NE]), ALU.add))
                    elif part == 1:
                        after(4)
                        done(nc.vector.tensor_reduce(r_1[:], r_b[:], AX.X, ALU.max))
                        after(5)
                        done(tt(r_a[:], r_b[:], spread(r_1[:], NE), ALU.subtract))
                        after(6)
                        done(ts(r_c[:], r_a[:], -1.0, None, ALU.add))
                        after(7)
                        done(nc.vector.reciprocal(r_a[:], r_c[:]))
                    elif part == 2:
                        after(8)
                        dve.wait_ge(rt_silu, n + 1)
                        done(tt(r_b[:], r_silu[:], r_a[:], ALU.mult))
                        after(9)
                        done(ts(r_a[:], r_b[:], -1.0, 1.0, ALU.mult, ALU.add))
                        after(10)
                        done(nc.vector.reciprocal(r_c[:], r_a[:]))
                        after(11)
                        done(tt(r_a[:], r_b[:], r_c[:], ALU.mult))
                    elif part == 3:
                        after(12)
                        done(nc.vector.tensor_reduce(r_2[:], r_a[:], AX.X, ALU.add))
                        after(13)
                        done(nc.vector.reciprocal(r_3[:], r_2[:]))
                        after(14)
                        done(tt(r_b[:], r_a[:], spread(r_3[:], NE), ALU.mult))
                        of_f = r_b[:].unsqueeze(2).broadcast_to([P, GT, NE, NE])
                        of_e = r_b[:].unsqueeze(3).broadcast_to([P, GT, NE, NE])
                        after(15)
                        done(tt(r_gt[:], of_f, of_e, ALU.is_gt))
                        done(tt(r_eq[:], of_f, of_e, ALU.is_equal))
                    elif part == 4:
                        after(17)
                        done(tt(r_eq[:], r_eq[:], lower[:].unsqueeze(1).broadcast_to([P, GT, NE, NE]), ALU.mult))
                        after(18)
                        done(tt(r_gt[:], r_gt[:], r_eq[:], ALU.add))
                        after(19)
                        done(nc.vector.tensor_reduce(r_a[:], r_gt[:], AX.X, ALU.add))
                        after(20)
                        done(stt(out=r_c[:], in0=r_a[:], scalar=float(TOPK), in1=r_b[:], op0=ALU.is_lt, op1=ALU.mult))
                    elif part == 5:
                        after(21)
                        done(nc.vector.tensor_reduce(r_1[:], r_c[:], AX.X, ALU.add))
                        after(22)
                        done(ts(r_2[:], r_1[:], TOPK_EPS, None, ALU.add))
                        after(23)
                        done(nc.vector.reciprocal(r_3[:], r_2[:]))
                        after(24)
                        done(tt(r_a[:], r_c[:], spread(r_3[:], NE), ALU.mult))
                        dve.wait_ge(route_turned, n)
                        after(25)
                        done(cp(route[:, :, 0:NE], r_a[:]))
                        after(26)
                        done(tt(route[:, :, 32:32 + NE], r_a[:], route[:, :, 0:NE].bitcast(F32), ALU.subtract))

                def product(g, s):
                    n = g * STEPS + (s + base)
                    dve.wait_ge(up_ready, n + 1)
                    dve.wait_ge(silu_ready, n + 1)
                    if not (ph == 0 and isinstance(g, int) and g == 0 and s < LAG):
                        dve.wait_ge(lo_ready, n - (LAG - 1))
                    if s < 2:
                        tt(h[:, s % LAG, :], silu[:, s % 2, :], bank(U_BANK[s % 2]), ALU.mult).then_inc(up_used, 1)
                    else:
                        dve.wait_ge(h_ready, g * (2 * NE) + (groups * 2 * NE + s - 2))
                        tt(act_up[:], silu[:, s % 2, :], bank(U_BANK[s % 2]), ALU.mult).then_inc(up_used, 1)
                        dve.wait_ge(bc_ready, g * NE + (groups * NE + s // 2))
                        dve.wait_ge(up_used, n + 1)
                        tt(h[:, s % LAG, :], act_up[:], bank(BC_BANK), ALU.mult).then_inc(h_ready, 1)

                def update(g, last_group):
                    dve.wait_ge(out_turned, g + groups + 1)
                    stt(out=of_group(x, g), in0=bank(BC_BANK if last_group else Z_BANK), scalar=0.5, in1=of_group(x, g),
                        op0=ALU.mult, op1=ALU.add).then_inc(x_updated, 1)

                def window(g, k0, k1, last):
                    for k in range(k0, k1):
                        if last and ph == 0:
                            attend(0, beside.get(k - 1, []))
                        product(*group_step(g, k))
                        if k < 2:
                            prep_route(g, 2 * k + 2)
                            prep_route(g, 2 * k + 3)
                        if ph == 0 and k < PRE:
                            split_expert(RAW + k)
                        if ph == 0 and k == PRE - 1:
                            for x_g in range(1, NG):
                                dve.wait_ge(in_x[x_g], 16)
                            keys_values()
                        if ph == 1 and k < RECIPS:
                            reciprocals(NG - 1, k)
                        if not last:
                            if k == AT_STATS:
                                prep_stats(g + 1)
                            if k == AT_NORM:
                                prep_norm(g + 1)
                            if k == AT_STATS2:
                                prep_stats2(g + 1)
                            if k == AT_SPLIT:
                                prep_round(g + 1)
                            if k in AT_ROUTE:
                                prep_route(g + 1, AT_ROUTE[k])
                            if k == AT_UPDATE:
                                update(g, False)
                    if last:
                        update(g, True)
                        if ph == 0:
                            attend(0, beside.get(STEPS - 1, []))

                def open_route():
                    prep_route(0, 0)
                    prep_route(0, 1)

                return {"stats": lambda: prep_stats(0), "norm": lambda: prep_norm(0), "stats2": lambda: prep_stats2(0),
                        "split": lambda: prep_round(0), "route": open_route, "run": lambda: ffn_windows(dve, window)}

            first, second = ffn(0), ffn(1)

            def split_expert(e):
                dve.wait_ge(w_rounded, e + 1)
                tt(w_lo[:, e, :], w_raw[:, e % RAW, :], w_hi[:, e, :].bitcast(F32), ALU.subtract).then_inc(w_split, 1)

            def keys_values():
                nc.vector.memset(k_parts[QROWS:P, :, :].bitcast(F32), 1.0).then_inc(k_split, 1)
                for i in range(HI):
                    dve.wait_ge(k_ready, 2 * i + 2)
                    tt(k_parts[32:64, i, :], k_fp[32:64, i, :], k_parts[32:64, i, :].bitcast(F32), ALU.subtract).then_inc(k_split, 1)

            def reciprocals(g, part):
                at = [GTOK * n // RECIPS // DH * DH for n in range(RECIPS + 1)]
                a, b = at[part], at[part + 1]
                dve.wait_ge(den_placed, g * PLACED + PLACED)
                nc.vector.reciprocal(rden[:, a:b], den[:, a:b]).then_inc(recip_done, 1)

            first["stats"]()
            first["norm"]()
            for e in range(NE):
                last = ts(expert_sel[:, e, :], ones[:], expert_ind[:, e:e + 1], None, ALU.mult)
            last.then_inc(sel_set, 1)
            dve.wait_ge(gates_summed, 1)
            cp(gate_sum[:].rearrange("p a e -> p (a e)"), psum[:, GS_BANK, 0:2 * NE]).then_inc(sums_read, 1)
            first["stats2"]()
            split_expert(0)
            first["split"]()
            dve.wait_ge(sums_read, 1)
            first["route"]()
            split_expert(1)
            split_expert(2)
            dve.wait_ge(in_k, IN_K)
            dve.wait_ge(v_projected, 1)
            tt(v_fp, bank(VP_BANK).rearrange("p (k c) -> p k c", k=KB), bv[:].unsqueeze(1).broadcast_to([P, KB, H]),
               ALU.add).then_inc(v_ready, 1)
            cp(wq_hi[:], wq_raw).then_inc(wq_rounded, 1)
            dve.wait_ge(wq_rounded, 1)
            tt(wq_lo[:], wq_raw, wq_hi[:].bitcast(F32), ALU.subtract).then_inc(wq_split, 1)

            def attend(g0, events):
                mt_use, _ = ring_uses(events)
                for ev in events:
                    kind = ev[0]
                    if kind == "NEXT" and ev[1] in second:
                        second[ev[1]]()
                    if kind == "M":
                        _, u, qt, j = ev
                        dve.wait_ge(m_filled, g0 * 64 + (16 * u + 4 * qt + j + 1))
                        nc.vector.tensor_reduce(neg_max[:, u % 2, qt, j:j + 1], bank(M_BANK[j % 2]), AX.X, ALU.max,
                                                negate=True).then_inc(m_freed, 1)
                        if qt == GT - 1 and j == HJ - 1:
                            dve.wait_ge(m_freed, g0 * 64 + 16 * (u + 1))
                            if u >= 1:
                                dve.wait_ge(s_filled, g0 * RING + (RING0 + mt_use[u - 1] + 1))
                            cp(max_stage[:, :, QROWS:QROWS + HJ], neg_max[:, u % 2]).then_inc(max_hi, 1)
                            dve.wait_ge(max_hi, g0 * HI + (u + 1))
                            tt(max_stage[:, :, QROWS + HJ:QROWS + 2 * HJ], neg_max[:, u % 2],
                               max_stage[:, :, QROWS:QROWS + HJ].bitcast(F32), ALU.subtract).then_inc(max_lo, 1)
                    elif kind == "LNS":
                        norm_stats(g0 + (ev[1] + NG), g0 + ev[1])
                    elif kind == "LNN":
                        g = g0 + ev[1]
                        dve.wait_ge(y_added, g)
                        norm(g + NG, g)
                    elif kind == "RECIP":
                        reciprocals(g0 + ev[1], ev[2])

            first["run"]()
            att_windows(dve, attend)
            second["run"]()

        @block.gpsimd
        def _(pool):
            nc.gpsimd.memset(minus_half[:], -0.5).then_inc(pool_set, 1)
            nc.gpsimd.memset(route[:].bitcast(F32), 0.0).then_inc(pool_set, 1)
            nc.gpsimd.memset(max_stage[:].bitcast(F32), 0.0).then_inc(pool_set, 1)
            nc.gpsimd.memset(v_pad[:], 0.0).then_inc(pool_set, 1)
            pool.wait_ge(pool_set, 4)
            for i in range(HI):
                c = 2 * DH + DH * (i % 2)
                nc.gpsimd.memset(v_pad[:, :, i, :, c:c + DH], 1.0).then_inc(pool_set, 1)
            pool.wait_ge(pool_set, POOL_SETS)

            def inverse_root(n, var_sem, out, out_sem):
                pool.wait_ge(var_sem, n * LN_VAR + LN_VAR)
                nc.gpsimd.tensor_tensor(out[:], var_eps[:], minus_half[:], ALU.pow).then_inc(out_sem, 1)

            def ffn(ph):
                base, groups = ph * NG * STEPS, ph * NG

                def prep_stats(g):
                    inverse_root(g + 2 * groups, ln_var, rstd, ln_rstd)

                def prep_norm(g):
                    inverse_root(g + groups, ln_var2, rstd2, ln_rstd2)

                def prep_split(g):
                    pool.wait_ge(z_rounded, g + groups + 1)
                    nc.gpsimd.tensor_tensor(of_group(zT_lo, g % 2), zT[:], of_group(zT_hi, g % 2).bitcast(F32),
                                            ALU.subtract).then_inc(z_split, 1)

                def split_h(g, s):
                    n = g * STEPS + (s + base)
                    pool.wait_ge(hi_ready, n + 1)
                    nc.gpsimd.tensor_tensor(h_lo[:, s % LAG, :], h[:, s % LAG, :], h_hi[:, s % LAG, :].bitcast(F32),
                                            ALU.subtract).then_inc(lo_ready, 1)

                def window(g, k0, k1, last):
                    for k in range(k0, k1):
                        if last and ph == 0:
                            attend(0, beside.get(k - 1, []))
                        if k >= 1:
                            split_h(*group_step(g, k - 1))
                        if not last:
                            if k == AT_STATS:
                                prep_stats(g + 1)
                            if k == AT_STATS2:
                                prep_norm(g + 1)
                            if k == AT_SPLIT:
                                prep_split(g + 1)
                        if ph == 1 and k == PRE - 1:
                            post(NG - 1)
                    if last:
                        split_h(g, STEPS - 1)
                        if ph == 0:
                            attend(0, beside.get(STEPS - 1, []))

                return {"stats": lambda: prep_stats(0), "stats2": lambda: prep_norm(0), "split": lambda: prep_split(0),
                        "run": lambda: ffn_windows(pool, window)}

            first, second = ffn(0), ffn(1)

            def attend(g0, events):
                for ev in events:
                    kind, use = ev[0], ev[-1]
                    if kind == "NEXT" and ev[1] in second:
                        second[ev[1]]()
                    if kind == "POST":
                        post(g0 + ev[1])
                    elif kind == "LNS":
                        inverse_root(g0 + (ev[1] + NG), ln_var, rstd, ln_rstd)
                    elif kind == "PROJ":
                        u = ev[1]
                        i = u % HI
                        pool.wait_ge(s_freed, g0 * RING + (RING0 + use + 1))
                        pool.wait_ge(q_rounded, g0 * HI + (u + 1))
                        nc.gpsimd.tensor_tensor(q_stack[0:32, i, :], q_fp[:, u % 2, :],
                                                q_stack[0:32, i, :].bitcast(F32), ALU.subtract).then_inc(q_ready, 1)
                    elif kind == "YT":
                        g, half = g0 + ev[1], ev[2]
                        cols = slice(2 * half * P, 2 * (half + 1) * P)
                        pool.wait_ge(s_freed, g0 * RING + (RING0 + use + 1))
                        pool.wait_ge(y_rounded, 2 * g + (half + 1))
                        nc.gpsimd.tensor_tensor(yT_lo[:, cols], zT[:, cols], yT_hi[:, cols].bitcast(F32),
                                                ALU.subtract).then_inc(y_split, 1)
                        if half == 1:
                            nc.gpsimd.tensor_tensor(of_group(x, g), of_group(x, g), z[:].rearrange("p t f -> p (t f)"),
                                                    ALU.add).then_inc(y_added, 1)

            def post(g):
                pool.wait_ge(recip_done, g * RECIPS + RECIPS)
                pool.wait_ge(num_placed, g * PLACED + PLACED)
                nc.gpsimd.tensor_tensor(num, num, rden, ALU.mult).then_inc(att_done, 1)
                pool.wait_ge(att_done, g + 1)
                pool.wait_ge(y_added, g + 1)
                for t in range(2):
                    xs = of_group(x, g).rearrange("p (b k t) -> p b k t", b=2, t=2)[:, :, :, t]
                    last = nc.gpsimd.tensor_tensor(xs, xs, num.rearrange("p (b t k) -> p b t k", b=2, t=2)[:, :, t, :], ALU.add)
                last.then_inc(x_attended, 1)

            first["stats"]()
            first["stats2"]()
            first["split"]()
            first["run"]()
            att_windows(pool, attend)
            second["run"]()


def kernel(L0_attn_queries, L0_attn_keys, L0_attn_values, L0_attn_Wq_w, L0_attn_Wq_b, L0_attn_Wk_w, L0_attn_Wk_b,
           L0_attn_Wv_w, L0_attn_Wv_b, L0_ffn_ln_scale, L0_ffn_ln_bias, L0_ffn_gate_w, L0_ffn_Wg, L0_ffn_Wu, L0_ffn_Wd,
           L0_ffn_sWg, L0_ffn_sWu, L0_ffn_sWd):
    import concourse.bacc as bacc
    from concourse.bass_utils import run_bass_kernel_spmd

    f32 = np.float32

    def arr(a):
        return np.ascontiguousarray(np.asarray(a))

    def stack_weights(w):
        w = arr(w).T.reshape(H, HJ, HI, DH).transpose(0, 2, 1, 3).reshape(H, HI, 1, HJ * DH)
        return np.ascontiguousarray(np.repeat(w, 3, axis=2).reshape(H, HI * QROWS))

    def stack_bias(b):
        b = arr(b).reshape(HJ, HI, DH).transpose(0, 2, 1).reshape(HJ * DH, HI)
        return np.ascontiguousarray(np.tile(b, (3, 1)))

    p = np.arange(P)
    copies = p[:, None] < QROWS
    head = np.where(copies, (p[:, None] % 32) // DH == np.arange(HJ), (p[:, None] - QROWS) % HJ == np.arange(HJ))
    head = head & (p[:, None] < QROWS + 2 * HJ)
    expert = (p[:, None] == np.arange(NE)) | (p[:, None] == 32 + np.arange(NE))
    lower = np.arange(NE)[None, :] < np.arange(NE)[:, None]
    arrays = {
        "x": arr(L0_attn_queries), "keysT": arr(arr(L0_attn_keys)[0].T), "valuesT": arr(arr(L0_attn_values)[0].T),
        "wq": stack_weights(L0_attn_Wq_w), "wk": stack_weights(L0_attn_Wk_w), "wvT": arr(arr(L0_attn_Wv_w).T),
        "bq": stack_bias(L0_attn_Wq_b), "bk": stack_bias(L0_attn_Wk_b),
        "bv": np.ascontiguousarray(np.tile(arr(L0_attn_Wv_b)[None, :], (P, 1))),
        "ln_scale": arr(L0_ffn_ln_scale).reshape(H, 1), "ln_bias": arr(L0_ffn_ln_bias).reshape(H, 1),
        "gate_t": arr(arr(L0_ffn_gate_w).T), "Wg": arr(L0_ffn_Wg), "Wu": arr(L0_ffn_Wu), "Wd": arr(L0_ffn_Wd),
        "sWg": arr(L0_ffn_sWg), "sWu": arr(L0_ffn_sWu), "sWd": arr(L0_ffn_sWd),
        "c_ident": np.eye(P, dtype=f32), "c_head": head.astype(f32), "c_expert": expert.astype(f32),
        "c_lower": np.ascontiguousarray(np.broadcast_to(lower.reshape(1, NE * NE), (P, NE * NE)).astype(f32)),
    }
    nc = bacc.Bacc("TRN2", target_bir_lowering=False, num_devices=1)
    d = {n: nc.dram_tensor(f"in_{n}", a.shape, mybir.dt.from_np(a.dtype), kind="ExternalInput").ap() for n, a in arrays.items()}
    d["out"] = nc.dram_tensor("out_x", (NB, S, H), F32, kind="ExternalOutput").ap()
    build(nc, d)
    r = run_bass_kernel_spmd(nc, [{f"in_{n}": a for n, a in arrays.items()}], core_ids=[0])
    return r.results[0]["out_x"]
```

```python
from contextlib import ExitStack

import numpy as np

import concourse.bass as bass
from concourse import mybir

F32 = mybir.dt.float32
F32R = mybir.dt.float32r
ALU = mybir.AluOpType
ACT = mybir.ActivationFunctionType
AX = mybir.AxisListType

P = 128
NB, S, H = 16, 256, 128
KEYS, NH, DH = 512, 16, 8
NE, TOPK, INTER = 8, 2, 256
LN_EPS, TOPK_EPS = 1e-5, 1e-5
GT = 4
GTOK = GT * P
NG = NB * S // GTOK
EXP = NE + 1
STEPS = 2 * EXP
KB = KEYS // P
HI, HJ = 4, 4
WCOLS = 2 * INTER + 2 * H
LAG = 3
PRE = 6
RAW = 3
QROWS = 96
LN_VAR = 7
RT, RT_SILU = 27, 7
RING_KINDS = ("S", "PROJ", "YT", "MT")
IN_G, IN_C, IN_K = 4 * 16, 3 * 16, 8 * 16
POOL_SETS = 8
NUM_MOVES, DEN_MOVES = 16 * 8, 16 * 4


def build(nc, d):
    with ExitStack() as ctx:
        def sb(name, shape, dt=F32):
            return ctx.enter_context(nc.sbuf_tensor(name, shape, dt))

        def sem(name):
            return ctx.enter_context(nc.semaphore(name))

        psum = ctx.enter_context(nc.psum_tensor("psum", [P, 8, 512], F32))

        x = sb("x", [P, NG, GTOK])
        ident = sb("ident", [P, P])
        w_hi = sb("w_hi", [P, EXP, WCOLS], F32R)
        w_lo = sb("w_lo", [P, EXP, WCOLS], F32R)
        k_stack = sb("k_stack", [P, HI, HJ, KEYS], F32R)
        v_pad = sb("v_pad", [P, KB, HI, HJ, 32])
        minus_half = sb("minus_half", [P, GT])
        neg_mean = sb("neg_mean", [P, GT])
        mean2 = sb("mean2", [P, GT])
        stats = sb("stats", [P, GT, 6])
        ln_tmp = sb("ln_tmp", [P, 5, GT])
        var_eps = sb("var_eps", [P, GT])
        rstd = sb("rstd", [P, GT])
        shift = sb("shift", [P, GT])
        rstd2 = sb("rstd2", [P, GT])
        z = sb("z", [P, GT, H])
        zT = sb("zT", [P, GTOK])
        staging = sb("staging", [P, RAW * WCOLS])
        w_raw = staging[:].rearrange("p (r c) -> p r c", r=RAW)
        zT_hi = sb("zT_hi", [P, 2, GTOK], F32R)
        zT_lo = sb("zT_lo", [P, 2, GTOK], F32R)
        gate_t = sb("gate_t", [P, NE])
        ln_scale = sb("ln_scale", [P, 1])
        ln_bias = sb("ln_bias", [P, 1])
        gate_s = sb("gate_s", [P, 2, NE])
        gate_sum = sb("gate_sum", [P, 2, NE])
        ones = sb("ones", [P, P])
        lower = sb("lower", [P, NE, NE])
        expert_ind = sb("expert_ind", [P, NE])
        expert_sel = sb("expert_sel", [P, NE, P], F32R)
        r_a = sb("r_a", [P, GT, NE])
        r_b = sb("r_b", [P, GT, NE])
        r_c = sb("r_c", [P, GT, NE])
        r_silu = sb("r_silu", [P, GT, NE])
        r_1 = sb("r_1", [P, GT])
        r_2 = sb("r_2", [P, GT])
        r_3 = sb("r_3", [P, GT])
        r_gt = sb("r_gt", [P, GT, NE, NE])
        r_eq = sb("r_eq", [P, GT, NE, NE])
        route = sb("route", [P, GT, P], F32R)
        route_T = sb("route_T", [P, 2, GTOK], F32R)
        silu = sb("silu", [P, 2, GTOK])
        act_up = sb("act_up", [P, GTOK])
        h = sb("h", [P, LAG, GTOK])
        h_hi = sb("h_hi", [P, LAG, GTOK], F32R)
        h_lo = sb("h_lo", [P, LAG, GTOK], F32R)
        out_T = sb("out_T", [P, GTOK])
        wq_hi = sb("wq_hi", [P, HI, QROWS], F32R)
        wq_lo = sb("wq_lo", [P, HI, QROWS], F32R)
        wk = sb("wk", [P, HI, QROWS])
        wvT = sb("wvT", [P, H])
        bq = sb("bq", [QROWS, HI])
        bk = sb("bk", [QROWS, HI])
        bv = sb("bv", [P, H])
        head_ind = sb("head_ind", [P, HJ])
        q_stack = sb("q_stack", [P, HI, GTOK], F32R)
        k_parts = q_stack
        yT_hi, yT_lo = zT_hi[:, 0, :], zT_lo[:, 0, :]
        q_fp = sb("q_fp", [32, 2, GTOK])
        neg_max = sb("neg_max", [P, 2, GT, HJ])
        max_stage = sb("max_stage", [P, GT, P], F32R)
        probs = sb("probs", [P, 2, HJ, GTOK])
        k_fp, keysT, valuesT = probs[0:QROWS, 0, :, :], probs[:, 1, 0, :], probs[:, 1, 1, :]
        v_fp = probs[:, 1, 2, :].rearrange("p (k c) -> p k c", k=KB)
        wq_raw = probs[:, 1, 3, 0:HI * QROWS].rearrange("p (i c) -> p i c", i=HI)
        acc_a, acc_b, num = (staging[:, n * GTOK:(n + 1) * GTOK] for n in range(3))
        rden = out_T[:]
        den_c = sb("den_c", [P, GTOK // DH])

        in_g, in_c, in_k = sem("in_gates"), sem("in_consts"), sem("in_attention")
        in_x = [sem(f"in_x{g}") for g in range(NG)]
        in_w = [sem(f"in_w{r}") for r in range(RAW)]
        gates_scaled, ones_set, pool_set, sel_set = sem("gates_scaled"), sem("ones_set"), sem("pool_set"), sem("sel_set")
        table_loaded = sem("table_loaded")
        w_rounded, w_split = sem("w_rounded"), sem("w_split")
        k_projected, v_projected, gates_summed = sem("k_projected"), sem("v_projected"), sem("gates_summed")
        k_ready, k_rounded, k_split, k_stacked = sem("k_ready"), sem("k_rounded"), sem("k_split"), sem("k_stacked")
        wq_rounded, wq_split, v_ready, v_padded, sums_read = (sem("wq_rounded"), sem("wq_split"), sem("v_ready"),
                                                              sem("v_padded"), sem("sums_read"))
        ln_stat, ln_var, ln_rstd, ln_shift, ln_done = sem("ln_stat"), sem("ln_var"), sem("ln_rstd"), sem("ln_shift"), sem("ln_done")
        ln_stat2, ln_var2, ln_rstd2 = sem("ln_stat2"), sem("ln_var2"), sem("ln_rstd2")
        z_turned, z_copied, z_rounded, z_split = sem("z_turned"), sem("z_copied"), sem("z_rounded"), sem("z_split")
        logits_ready, rt_step, rt_silu = sem("logits_ready"), sem("rt_step"), sem("rt_silu")
        route_turned, route_copied = sem("route_turned"), sem("route_copied")
        gate_ready, up_ready, bc_ready, down_done = sem("gate_ready"), sem("up_ready"), sem("bc_ready"), sem("down_done")
        silu_ready, up_used, h_ready = sem("silu_ready"), sem("up_used"), sem("h_ready")
        hi_ready, lo_ready = sem("hi_ready"), sem("lo_ready")
        out_copied, out_turned, x_updated = sem("out_copied"), sem("out_turned"), sem("x_updated")
        s_filled, s_freed = sem("s_filled"), sem("s_freed")
        m_filled, m_freed = sem("m_filled"), sem("m_freed")
        q_rounded, q_ready = sem("q_rounded"), sem("q_ready")
        y_rounded, y_split, y_added = sem("y_rounded"), sem("y_split"), sem("y_added")
        max_hi, max_lo = sem("max_hi"), sem("max_lo")
        av_done, acc_copied = sem("av_done"), sem("acc_copied")
        num_placed, den_placed = sem("num_placed"), sem("den_placed")
        recip_stored, rden_placed = sem("recip_stored"), sem("rden_placed")
        recip_done, att_done, x_attended = sem("recip_done"), sem("att_done"), sem("x_attended")
        stored = sem("stored")

        G_BANK, U_BANK, BC_BANK, OUT_BANK, Z_BANK, R_BANK = (0, 1), (2, 3), 4, 5, 6, 7
        S_BANK, ACC_BANK, M_BANK = (0, 2), 4, (6, 7, 5)
        GS_BANK = 5

        def bank(b, rows=P):
            return psum[0:rows, b, :]

        def of_group(buf, g):
            return buf[:, bass.ds(g, 1), :].rearrange("p a n -> p (a n)")

        block = ctx.enter_context(nc.Block())

        def ffn_windows(eng, window, ph):
            window(0, 0, PRE, False)
            if ph == 0:
                window(0, PRE, PRE + STEPS, False)
            with eng.Fori(1 - ph, NG - 1) as g:
                window(g, PRE, PRE + STEPS, False)
            window(NG - 1, PRE, STEPS, True)

        def is_first(g):
            return isinstance(g, int) and g == 0

        def expert_at(k):
            return RAW - 1 if k == 0 else RAW + k // 2 if k % 2 == 1 and k < 2 * (EXP - RAW) else None

        def group_step(g, k):
            return (g + 1, k - STEPS) if k >= STEPS else (g, k)

        AT_STATS, AT_VAR, AT_STATS2, AT_VAR2 = 12, 14, 19, 21
        AT_NORM, AT_COPY, AT_ROUTE_SILU = 17, 20, 28
        AT_RSTD, AT_TURN, AT_SPLIT, AT_RSTD2, AT_LOGITS = 7, 10, 10, 11, 11
        AT_ROUTE, ROUTE_PARTS = 24, 14
        AT_ROUTE_TURN, AT_ROUTE_COPY = 19, 20
        STACK_AT = [0, 2, *range(4, 12), *range(12, 24, 2)]
        AT_KEYS, AT_VALUES, AT_PARTS = 11, 20, 18
        AT_OUT, AT_OUT_TURN, AT_UPDATE = STEPS + LAG, STEPS + LAG + 1, STEPS + LAG + 2

        AV_LAG = 2
        AT_RECIP, AT_POST = 3, 8
        FIRST, PER_GROUP = HI * KB, HI * KB

        def att_events(k, end):
            dg, r = divmod(k, HI * KB)
            i, kb = divmod(r, KB)
            u = HI * dg + i
            ahead = u + (2 if kb == KB - 1 else 1)
            m = [] if ahead >= HI * end else [("M", ahead, (kb + 1) % GT, j) for j in range(HJ)]
            out = m[:2]
            if dg + 1 < end:
                norm = {0: ("LNS", 0), 1: ("LNS", 1), 2: ("LNS", 2), 3: ("LNS", 3), 5: ("LNN", 0), 6: ("LNN", 1), 7: ("YT", 0), 8: ("YT", 1)}
                out += [(name, dg + 1, part) for name, part in [norm[r]]] if r in norm else []
            if kb == (1 if i == HI - 2 else 0) and u + 2 < HI * end:
                out += [("PROJ", u + 2)]
            out += [("AV", k - AV_LAG)]
            if kb == KB - 1 and u + 1 < HI * end:
                out += [("MT", u + 1)]
            if r % (2 * KB) == AV_LAG - 1:
                out += [("EVAC", 2 * dg + i // 2 - 1)]
            out += m[2:3] + [("SA", u, kb, 0)] + [("S", u, kb, 0)] + m[3:] + [("SA", u, kb, 1)] + [("S", u, kb, 1)]
            if r == AT_RECIP:
                out += [("RECIP", dg - 1)]
            if r == AT_POST:
                out += [("POST", dg - 1)]
            return out

        def number(events, start):
            out = []
            for ev in events:
                out.append((*ev, start) if ev[0] in RING_KINDS or ev[0] == "SA" else ev)
                start += ev[0] in RING_KINDS
            return out

        EARLY_USES = 4
        first_maxima = [("M", u, qt, j) for u in range(2) for qt in range(GT) for j in range(HJ)][:20]
        beside = {5: [("LNS", 0, part) for part in range(4)], 6: [("LNN", 0, 0), ("LNN", 0, 1)],
                  8: [("YT", 0, 0), ("YT", 0, 1)], 10: [("PROJ", 0), ("PROJ", 1)]}
        beside.update({k: first_maxima[2 * (k - 11):2 * (k - 10)] for k in range(11, STEPS + 2)})
        EARLY_MAXIMA = 2 * (STEPS + 2 - 11)
        opening = [("MT", 0)] + first_maxima[EARLY_MAXIMA:]
        opening += [e for k in range(FIRST) for e in att_events(k, NG)
                    if not (e[0] in ("AV", "EVAC", "RECIP", "POST") and e[1] < 0)]
        RING0 = EARLY_USES + sum(e[0] in RING_KINDS for e in opening)
        opening = number(opening, EARLY_USES - RING0)
        uses = -RING0
        for k, events in beside.items():
            beside[k] = number(events, uses)
            uses += sum(e[0] in RING_KINDS for e in events)
        middle = number([e for k in range(FIRST, FIRST + PER_GROUP) for e in att_events(k, NG)], 0)
        RING = sum(e[0] in RING_KINDS for e in middle)
        final = [e for k in range(FIRST, FIRST + PER_GROUP) for e in att_events(k, 2)]
        for k, names in {1: ["stats"], 4: ["norm"], 6: ["stats2"], 12: ["turn", "copy", "split"], 13: ["logits", "route"],
                         14: ["exp"]}.items():
            at = final.index(("AV", FIRST + k - AV_LAG)) + 1
            final[at:at] = [("NEXT", name) for name in names]
        final = number(final + [("AV", FIRST + PER_GROUP - n) for n in range(AV_LAG, 0, -1)] + [("EVAC", 3), ("NEXT", "turn_route"), ("NEXT", "copy_route")], 0)
        RING_END = sum(e[0] in RING_KINDS for e in final)
        assert RING % 2 == 0

        def ring_uses(events):
            mt, sc = {}, {}
            for ev in opening + (events if events is not opening else []):
                if ev[0] == "MT":
                    mt[ev[1]] = ev[-1]
                if ev[0] == "S" and ev[3] == 1:
                    sc[ev[1] * KB + ev[2]] = ev[-1]
            return mt, sc

        def ring_bank(use):
            if use < EARLY_USES - RING0:
                return (Z_BANK, R_BANK)[(RING0 + use) % 2]
            return S_BANK[(RING0 + use) % 2]

        def m_bank(r, first):
            def of(r):
                if first and r < EARLY_MAXIMA:
                    return M_BANK[r % 2]
                return M_BANK[1 if r % 64 == 63 else r % 64 % 3]
            return of(r), next((q for q in range(r - 1, -1, -1) if of(q) == of(r)), None)

        def att_windows(eng, window):
            window(0, opening)
            with eng.Fori(0, NG - 2) as g:
                window(g, middle)
            window(NG - 2, final)

        def load_expert(eng, e):
            if e >= RAW:
                eng.wait_ge(w_split, e - RAW + 1)
            wg, wu, wd = (d["sWg"], d["sWu"], d["sWd"]) if e == 0 else (d["Wg"][e - 1], d["Wu"][e - 1], d["Wd"][e - 1])
            r = e % RAW
            eng.dma_start(w_raw[:, r, 0:INTER], wg).then_inc(in_w[r], 16)
            eng.dma_start(w_raw[:, r, INTER:2 * INTER], wu).then_inc(in_w[r], 16)
            eng.dma_start(w_raw[:, r, 2 * INTER:].rearrange("p (i n) -> p i n", i=2),
                          wd.rearrange("(i p) n -> p i n", i=2)).then_inc(in_w[r], 16)

        @block.sync
        def _(sp):
            def load_x(g):
                sp.dma_start(x[:, g, :].rearrange("p (b n) -> p b n", b=2),
                             d["x"][2 * g:2 * g + 2].rearrange("b (p t) f -> p b (t f)", t=2)).then_inc(in_x[g], 16)

            def load(to, of, done):
                sp.dma_start(to, d[of]).then_inc(done, 16)

            load_x(0)
            for to, of in ((ident[:], "c_ident"), (gate_t[:], "gate_t"), (ln_scale[:], "ln_scale"), (ln_bias[:], "ln_bias")):
                load(to, of, in_g)
            load(expert_ind[:], "c_expert", in_c)
            load(lower[:].rearrange("p e f -> p (e f)"), "c_lower", in_c)
            load(head_ind[:], "c_head", in_c)
            load_expert(sp, 1)
            load_expert(sp, 2)
            for to, of in ((wk[:].rearrange("p i c -> p (i c)"), "wk"), (keysT, "keysT"), (wvT[:], "wvT"), (valuesT, "valuesT"),
                           (wq_raw.rearrange("p i c -> p (i c)"), "wq"), (bq[:], "bq"), (bk[:], "bk"), (bv[:], "bv")):
                load(to, of, in_k)
            load_x(1)
            for e in range(RAW, EXP):
                load_expert(sp, e)
            for g in range(2, NG):
                load_x(g)

            half = 2 * DH
            def place(g):
                if not is_first(g):
                    sp.wait_ge(x_attended, g)
                for n, of in ((0, acc_a), (1, acc_b)):
                    sp.wait_ge(acc_copied, 2 * g + (n + 1))
                    for i in range(2):
                        to = (2 * n + i) * HJ * DH
                        sp.dma_start(den_c[to:to + HJ * DH, :],
                                     of[half + DH * i:P:2 * half, :]).then_inc(den_placed, 16)
                    for j in range(HJ):
                        sp.dma_start(num[32 * j + n * half:32 * j + (n + 1) * half, :],
                                     of[32 * j:32 * j + half, :]).then_inc(num_placed, 16)
                sp.wait_ge(recip_done, g + 1)
                sp.dma_start(d["recip"].rearrange("i j (e f) -> (i j e) f", e=DH), den_c[:]).then_inc(recip_stored, 16)
                sp.wait_ge(recip_stored, g * 16 + 16)
                for j in range(HJ):
                    sp.dma_start(rden[32 * j:32 * j + 32, :],
                                 d["recip"][:, j, :].unsqueeze(1).broadcast_to([HI, DH, GTOK])).then_inc(rden_placed, 16)

            place(0)
            with sp.Fori(1, NG) as g:
                place(g)
            with sp.Fori(0, NG) as g:
                sp.wait_ge(x_updated, g + (NG + 1))
                for b in range(2):
                    sp.dma_start(d["out"][bass.ds(2 * g + b, 1)].rearrange("b (p t) f -> (b p) (t f)", t=2),
                                 x[:, bass.ds(g, 1), b * S:(b + 1) * S].rearrange("p a n -> p (a n)")).then_inc(stored, 16)
            sp.wait_ge(stored, 16 * NB)

        @block.tensor
        def _(pe):
            mm = nc.tensor.matmul

            def three(out, w, wl, m, ml, start, stop):
                mm(out, w, m, start=start, stop=False)
                mm(out, w, ml, start=False, stop=False)
                return mm(out, wl, m, start=False, stop=stop)

            def turn(out, in_):
                return nc.tensor.transpose(out, in_, ident[:])

            pe.wait_ge(in_g, IN_G)
            pe.wait_ge(ones_set, 1)
            pe.wait_ge(gates_scaled, 2)
            mm(psum[:, GS_BANK, 0:2 * NE], ones[:], gate_s[:].rearrange("p a e -> p (a e)"),
               start=True, stop=True).then_inc(gates_summed, 1)

            def ffn(ph):
                base, groups = ph * NG * STEPS, ph * NG

                def prep_z(g):
                    pe.wait_ge(ln_done, g + 2 * groups + 1)
                    if not is_first(g):
                        pe.wait_ge(x_updated, g + groups - 1)
                    for t in range(GT):
                        last = turn(psum[:, Z_BANK, t * P:(t + 1) * P], z[:, t, :])
                    last.then_inc(z_turned, 1)

                def prep_logits(g):
                    pe.wait_ge(z_copied, g + groups + 1)
                    pe.wait_ge(route_copied, g + groups)
                    for t in range(GT):
                        last = mm(psum[:, R_BANK, t * NE:(t + 1) * NE], zT[:, t * P:(t + 1) * P], gate_s[:, 0, :],
                                  start=True, stop=True)
                    last.then_inc(logits_ready, 1)

                def turn_route(g):
                    pe.wait_ge(rt_step, g * RT + (groups * RT + RT))
                    for t in range(GT):
                        last = turn(psum[:, R_BANK, t * P:(t + 1) * P], route[:, t, :].bitcast(F32))
                    last.then_inc(route_turned, 1)

                def project_keys(i):
                    pe.wait_ge(in_k, IN_K)
                    if i == 0:
                        pe.wait_ge(z_copied, 2)
                    else:
                        pe.wait_ge(k_ready, 2 * i)
                    mm(bank(Z_BANK, QROWS), wk[:, i, :], keysT, start=True, stop=True).then_inc(k_projected, 1)

                def project_values():
                    pe.wait_ge(k_ready, 2 * HI)
                    for kb in range(KB):
                        last = mm(psum[:, Z_BANK, kb * H:(kb + 1) * H], valuesT[:, kb * P:(kb + 1) * P], wvT[:],
                                  start=True, stop=True)
                    last.then_inc(v_projected, 1)

                def gate_up(g, s):
                    n = g * STEPS + (s + base)
                    e, i = divmod(s, 2)
                    opens = ph == 0 and is_first(g) and s < 2
                    zh, zl = of_group(zT_hi, g % 2), of_group(zT_lo, g % 2)
                    if s == 0:
                        pe.wait_ge(z_split, g + groups + 1)
                    if ph == 0 and is_first(g):
                        pe.wait_ge(w_split, e + 1)
                    if not opens:
                        pe.wait_ge(silu_ready, n - 1)
                    c = i * P
                    three(bank(G_BANK[s % 2]), w_hi[:, e, c:c + P], w_lo[:, e, c:c + P], zh, zl,
                          True, True).then_inc(gate_ready, 1)
                    if not opens:
                        pe.wait_ge(up_used, n - 1)
                    c = INTER + i * P
                    three(bank(U_BANK[s % 2]), w_hi[:, e, c:c + P], w_lo[:, e, c:c + P], zh, zl,
                          True, True).then_inc(up_ready, 1)

                def down(g, s):
                    n = g * STEPS + (s + base)
                    e, i = divmod(s, 2)
                    pe.wait_ge(lo_ready, n + 1)
                    if s == 0:
                        pe.wait_ge(out_copied, g + groups)
                    if ph == 1 and is_first(g) and s == 0:
                        pe.wait_ge(acc_copied, 2 * NG)
                    c = 2 * INTER + i * H
                    three(bank(OUT_BANK), w_hi[:, e, c:c + H], w_lo[:, e, c:c + H], h_hi[:, s % LAG, :],
                          h_lo[:, s % LAG, :], s == 0, s == STEPS - 1).then_inc(down_done, 1)

                def broadcast(g, s):
                    e = s // 2 - 1
                    if ph == 0 and e == 0:
                        pe.wait_ge(sel_set, 1)
                    if e == 0:
                        pe.wait_ge(route_copied, g + groups + 1)
                    pe.wait_ge(h_ready, g * (2 * NE) + (groups * 2 * NE + 2 * e))
                    mm(bank(BC_BANK), expert_sel[:, e, :], of_group(route_T, g % 2),
                       start=True, stop=True).then_inc(bc_ready, 1)

                def finish(g, last_group):
                    pe.wait_ge(out_copied, g + groups + 1)
                    if last_group:
                        pe.wait_ge(h_ready, (groups + NG) * 2 * NE)
                    else:
                        pe.wait_ge(z_copied, g + groups + 2)
                    if ph == 0 and is_first(g):
                        pe.wait_ge(v_ready, 1)
                    for t in range(GT):
                        last = turn(psum[:, BC_BANK if last_group else Z_BANK, t * P:(t + 1) * P], out_T[:, t * P:(t + 1) * P])
                    last.then_inc(out_turned, 1)

                def window(g, k0, k1, last):
                    for k in range(k0, k1):
                        gg, s = group_step(g, k)
                        gate_up(gg, s)
                        if not last and k == AT_TURN:
                            prep_z(g + 1)
                        if k >= LAG:
                            down(*group_step(g, k - LAG))
                        if ph == 0 and k == 2:
                            turn_route(g)
                        if s >= 2 and s % 2 == 0:
                            broadcast(gg, s)
                        if not last:
                            if k == AT_LOGITS:
                                prep_logits(g + 1)
                            if k == AT_ROUTE_TURN:
                                turn_route(g + 1)
                            if k == AT_OUT_TURN:
                                finish(g, False)
                        if ph == 0 and is_first(g):
                            if k in range(AT_KEYS, AT_KEYS + 2 * HI, 2):
                                project_keys((k - AT_KEYS) // 2)
                            if k == AT_VALUES:
                                project_values()
                        if last and ph == 0:
                            attend(0, beside.get(k, []))
                    if last:
                        for k in range(STEPS, STEPS + LAG):
                            down(g, k - LAG)
                            if ph == 0:
                                attend(0, beside.get(k, []))
                        finish(g, True)

                def run():
                    if ph == 1:
                        pe.wait_ge(s_freed, RING * (NG - 2) + RING0 + RING_END)
                    ffn_windows(pe, window, ph)

                return {"turn": lambda: prep_z(0), "logits": lambda: prep_logits(0), "turn_route": lambda: turn_route(0), "run": run}

            first, second = ffn(0), ffn(1)
            def attend(g0, events):
                mt_use, s_use = ring_uses(events)

                def claim(use):
                    if use >= 2 - RING0:
                        pe.wait_ge(s_freed, g0 * RING + (RING0 + use - 1))
                    return ring_bank(use)

                for ev in events:
                    kind, use = ev[0], ev[-1]
                    if kind == "NEXT" and ev[1] == "turn":
                        pe.wait_ge(m_freed, 64 * NG)
                    if kind == "NEXT" and ev[1] in second:
                        second[ev[1]]()
                    if kind == "SA":
                        _, u, kb, jp, _ = ev
                        i = u % HI
                        if kb == 0 and jp == 0:
                            pe.wait_ge(s_freed, g0 * RING + (RING0 + mt_use[u] + 1))
                        mm(bank(claim(use)), k_stack[:, i, 2 * jp, kb * P:(kb + 1) * P], q_stack[:, i, :], start=True, stop=True)
                    elif kind == "S":
                        _, u, kb, jp, _ = ev
                        i = u % HI
                        mm(bank(ring_bank(use) + 1), k_stack[:, i, 2 * jp + 1, kb * P:(kb + 1) * P], q_stack[:, i, :],
                           start=True, stop=True).then_inc(s_filled, 1)
                    elif kind == "M":
                        _, u, qt, j = ev
                        i = u % HI
                        if qt == 0 and j == 0:
                            pe.wait_ge(q_ready, g0 * HI + (u + 1))
                        r = 16 * u + 4 * qt + j
                        if is_first(g0) and u < HI and qt == 0 and j == 0:
                            pe.wait_ge(k_stacked, HJ * (u + 1))
                        if r == 0:
                            pe.wait_ge(s_freed, EARLY_USES)
                        b, before = m_bank(r, is_first(g0))
                        if before is None and b == OUT_BANK:
                            pe.wait_ge(out_copied, NG)
                        elif before is not None:
                            pe.wait_ge(m_freed, g0 * 64 + (before + 1))
                        mm(bank(b), q_stack[0:QROWS, i, qt * P:(qt + 1) * P], k_stack[0:QROWS, i, j, :],
                           start=True, stop=True).then_inc(m_filled, 1)
                    elif kind == "PROJ":
                        i = ev[1] % HI
                        if i == 0:
                            pe.wait_ge(y_split, g0 * 2 + 2 * (ev[1] // HI + 1))
                        if use == 2 - RING0:
                            pe.wait_ge(wq_split, 1)
                        three(bank(claim(use), QROWS), wq_hi[:, i, :], wq_lo[:, i, :], yT_hi, yT_lo,
                              True, True).then_inc(s_filled, 1)
                    elif kind == "YT":
                        _, dg, half, _ = ev
                        pe.wait_ge(ln_done, g0 + (dg + NG + 1))
                        b = claim(use)
                        for t in range(2):
                            last = turn(psum[:, b, t * P:(t + 1) * P], z[:, 2 * half + t, :])
                        last.then_inc(s_filled, 1)
                    elif kind == "MT":
                        pe.wait_ge(max_lo, g0 * HI + (ev[1] + 1))
                        if use == EARLY_USES - RING0:
                            pe.wait_ge(silu_ready, NG * STEPS)
                            pe.wait_ge(up_used, NG * STEPS)
                        b = claim(use)
                        for t in range(GT):
                            last = turn(psum[:, b, t * P:(t + 1) * P], max_stage[:, t, :].bitcast(F32))
                        last.then_inc(s_filled, 1)
                    elif kind == "AV":
                        k = ev[1]
                        dg, r = divmod(k, HI * KB)
                        i, kb = divmod(r, KB)
                        pe.wait_ge(s_freed, g0 * RING + (RING0 + s_use[k] + 1))
                        if is_first(g0) and k == 0:
                            pe.wait_ge(x_updated, NG)
                            pe.wait_ge(v_padded, HI)
                        if kb == 0 and i % 2 == 0 and k > 0:
                            pe.wait_ge(acc_copied, g0 * 2 + (2 * dg + i // 2))
                        for j in range(HJ):
                            last = mm(psum[32 * j:32 * j + 32, ACC_BANK, :],
                                      v_pad[:, kb, i, j, :], probs[:, kb % 2, j, :],
                                      start=(i % 2 == 0 and kb == 0), stop=(i % 2 == 1 and kb == KB - 1))
                        last.then_inc(av_done, 1)

            first["turn"]()
            first["logits"]()
            pe.wait_ge(sums_read, 1)
            first["run"]()
            att_windows(pe, attend)
            second["run"]()

        @block.scalar
        def _(act):
            load_expert(act, 0)
            act.wait_ge(pool_set, 1)
            nc.scalar.activation(r_1[:], minus_half[:], ACT.Silu).then_inc(table_loaded, 1)

            def round_expert(e):
                act.wait_ge(in_w[e % RAW], 48 * (e // RAW + 1))
                nc.scalar.copy(w_hi[:, e, :], w_raw[:, e % RAW, :]).then_inc(w_rounded, 1)

            def normalise(g, half):
                for t in (2 * half, 2 * half + 1):
                    last = nc.scalar.activation(z[:, t, :], of_group(x, g)[:, t * H:(t + 1) * H], ACT.Identity,
                                                bias=shift[:, t:t + 1], scale=rstd[:, t:t + 1])
                if half == 1:
                    last.then_inc(ln_done, 1)

            def ffn(ph):
                base, groups = ph * NG * STEPS, ph * NG

                def norm(g, half):
                    act.wait_ge(ln_shift, g + (2 * groups + 1))
                    act.wait_ge(z_turned, g + groups)
                    act.wait_ge(ln_var2, g * LN_VAR + groups * LN_VAR)
                    if ph == 1:
                        act.wait_ge(y_added, NG)
                    normalise(g, half)

                def copy_z(g, part):
                    act.wait_ge(z_turned, g + groups + 1)
                    if part == 0:
                        nc.scalar.copy(of_group(zT_hi, g % 2), bank(Z_BANK)).then_inc(z_rounded, 1)
                        return
                    act.wait_ge(z_split, g + groups)
                    act.wait_ge(logits_ready, g + groups)
                    if ph == 1:
                        act.wait_ge(y_split, 2 * NG)
                    nc.scalar.copy(zT[:], bank(Z_BANK)).then_inc(z_copied, 1)

                def route_silu(g, func=ACT.Silu):
                    act.wait_ge(rt_step, g * RT + (groups * RT + RT_SILU))
                    nc.scalar.activation(r_silu[:], r_c[:], func).then_inc(rt_silu, 1)

                def prepare(g, place):
                    if place - AT_NORM in (0, 1):
                        norm(g, place - AT_NORM)
                    if place - AT_COPY in (0, 1):
                        copy_z(g, place - AT_COPY)
                    if place == AT_ROUTE_SILU:
                        route_silu(g)

                def stack_keys(place):
                    if place in STACK_AT:
                        i, j = divmod(STACK_AT.index(place), HJ)
                        nc.scalar.activation(k_stack[:, i, j, :], k_parts[:, i, :].bitcast(F32), ACT.Copy,
                                             scale=head_ind[:, j:j + 1]).then_inc(k_stacked, 1)

                def copy_route(g):
                    act.wait_ge(route_turned, g + groups + 1)
                    nc.scalar.copy(of_group(route_T, g % 2), bank(R_BANK)).then_inc(route_copied, 1)

                def copy_out(g):
                    act.wait_ge(down_done, g * STEPS + (base + STEPS))
                    act.wait_ge(out_turned, g + groups)
                    nc.scalar.copy(out_T[:], bank(OUT_BANK)).then_inc(out_copied, 1)

                def gates(g, s):
                    n = g * STEPS + (s + base)
                    act.wait_ge(gate_ready, n + 1)
                    if not (ph == 0 and is_first(g) and s < 2):
                        act.wait_ge(up_used, n - 1)
                    nc.scalar.activation(silu[:, s % 2, :], bank(G_BANK[s % 2]), ACT.Silu).then_inc(silu_ready, 1)

                def round_h(g, s):
                    n = g * STEPS + (s + base)
                    if s < 2:
                        act.wait_ge(up_used, n + 1)
                    else:
                        act.wait_ge(h_ready, g * (2 * NE) + (groups * 2 * NE + s - 1))
                    if not (ph == 0 and is_first(g) and s < LAG):
                        act.wait_ge(down_done, n - (LAG - 1))
                    nc.scalar.copy(h_hi[:, s % LAG, :], h[:, s % LAG, :]).then_inc(hi_ready, 1)

                def window(g, k0, k1, last):
                    for k in range(k0, k1):
                        if last and ph == 0:
                            attend(0, beside.get(k - 1, []))
                            if k == PRE:
                                act.wait_ge(k_split, HI + 1)
                                act.wait_ge(in_c, IN_C)
                        if k == AT_OUT:
                            copy_out(g)
                        if not last and k == AT_ROUTE_COPY:
                            copy_route(g + 1)
                        gates(*group_step(g, k))
                        if last and ph == 0:
                            stack_keys(2 * (k - PRE))
                        if not last:
                            prepare(g + 1, 2 * k)
                        if k >= 1:
                            round_h(*group_step(g, k - 1))
                        if last and ph == 0:
                            stack_keys(2 * (k - PRE) + 1)
                        if ph == 0 and k == 2:
                            copy_route(g)
                        if ph == 0 and is_first(g):
                            if expert_at(k) is not None:
                                round_expert(expert_at(k))
                            if 0 <= k - AT_KEYS - 1 < 2 * HI:
                                i, part = divmod(k - AT_KEYS - 1, 2)
                                act.wait_ge(in_k, IN_K)
                                act.wait_ge(k_projected, i + 1)
                                act.wait_ge(k_split, 1)
                                nc.scalar.activation(k_parts[0:QROWS, i, :] if part else k_fp[:, i, :], bank(Z_BANK, QROWS),
                                                     ACT.Relu, bias=bk[:, i:i + 1]).then_inc(k_ready, 1)
                            if k == AT_VALUES + 3:
                                act.wait_ge(v_ready, 1)
                                act.wait_ge(pool_set, POOL_SETS)
                                v_heads = v_fp.rearrange("p k (j i c) -> p k i j c", i=HI, j=HJ)
                                for i in range(HI):
                                    c = DH * (i % 2)
                                    nc.scalar.activation(v_pad[:, :, i, :, c:c + DH], v_heads[:, :, i, :, :],
                                                         ACT.Relu).then_inc(v_padded, 1)
                        if not last:
                            prepare(g + 1, 2 * k + 1)
                    if last:
                        round_h(g, STEPS - 1)
                        copy_out(g)

                def open_norm():
                    for half in range(2):
                        norm(0, half)

                def open_copy():
                    for part in range(2):
                        copy_z(0, part)

                return {"norm": open_norm, "copy": open_copy, "silu": lambda: route_silu(0), "exp": lambda: route_silu(0, ACT.Exp), "copy_route": lambda: copy_route(0), "run": lambda: ffn_windows(act, window, ph)}

            first, second = ffn(0), ffn(1)

            def attend(g0, events):
                for ev in events:
                    kind, use = ev[0], ev[-1]
                    if kind == "NEXT" and ev[1] in second:
                        second[ev[1]]()
                    if kind in RING_KINDS:
                        act.wait_ge(s_filled, g0 * RING + (RING0 + use + 1))
                        b = ring_bank(use)
                    if kind == "LNN":
                        g = g0 + ev[1]
                        if ev[2] == 0:
                            act.wait_ge(ln_shift, g + (NG + 1))
                            act.wait_ge(y_added, g)
                        normalise(g, ev[2])
                    elif kind == "S":
                        _, u, kb, jp, _ = ev
                        k = u * KB + kb
                        if k >= 2 and jp == 0:
                            act.wait_ge(av_done, g0 * 16 + (k - 1))
                        nc.scalar.activation(probs[:, kb % 2, 2 * jp:2 * jp + 2, :], psum[:, b:b + 2, :], ACT.Exp,
                                             scale=float(DH) ** -0.5).then_inc(s_freed, 1)
                    elif kind == "PROJ":
                        u = ev[1]
                        if u >= 2:
                            act.wait_ge(q_ready, g0 * HI + (u - 1))
                        if is_first(g0) and u < HI:
                            act.wait_ge(k_stacked, HJ * (u + 1))
                        nc.scalar.activation(q_stack[0:QROWS, u % HI, :], bank(b, QROWS), ACT.Relu,
                                             bias=bq[:, u % HI:u % HI + 1]).then_inc(q_rounded, 1)
                        nc.scalar.activation(q_fp[:, u % 2, :], psum[0:32, b, :], ACT.Relu,
                                             bias=bq[0:32, u % HI:u % HI + 1]).then_inc(s_freed, 1)
                    elif kind == "YT":
                        _, dg, half, _ = ev
                        act.wait_ge(y_split, g0 * 2 + 2 * dg)
                        cols = slice(2 * half * P, 2 * (half + 1) * P)
                        nc.scalar.copy(yT_hi[:, cols], psum[:, b, 0:2 * P]).then_inc(y_rounded, 1)
                        nc.scalar.copy(zT[:, cols], psum[:, b, 0:2 * P]).then_inc(s_freed, 1)
                    elif kind == "MT":
                        nc.scalar.copy(q_stack[QROWS:P, ev[1] % HI, :], psum[QROWS:P, b, :]).then_inc(s_freed, 1)
                    elif kind == "EVAC":
                        n = ev[1]
                        act.wait_ge(av_done, g0 * 16 + 8 * (n + 1))
                        if n > 0:
                            act.wait_ge(num_placed, g0 * NUM_MOVES + n * (NUM_MOVES // 2))
                            act.wait_ge(den_placed, g0 * DEN_MOVES + n * (DEN_MOVES // 2))
                        nc.scalar.copy(acc_b if n % 2 else acc_a, bank(ACC_BANK)).then_inc(acc_copied, 1)

            first["norm"]()
            round_expert(0)
            first["copy"]()
            round_expert(1)
            first["silu"]()
            first["run"]()
            att_windows(act, attend)
            second["run"]()

        @block.vector
        def _(dve):
            tt, ts = nc.vector.tensor_tensor, nc.vector.tensor_scalar
            stt, cp = nc.vector.scalar_tensor_tensor, nc.vector.tensor_copy

            def spread(v, n):
                return v.unsqueeze(2).broadcast_to([P, GT, n])

            nc.vector.memset(ones[:], 1.0).then_inc(ones_set, 1)
            def moments(rows, stat_sem, tiles=range(GT)):
                for t in tiles:
                    nc.vector.bn_stats(stats[:, t, :], rows[:, t * H:(t + 1) * H]).then_inc(stat_sem, 1)

            def variance_part(n, stat_sem, var_sem, mean_out, part):
                mean_e, mean_o, m2_e, m2_o = (stats[:, :, c] for c in (1, 4, 2, 5))
                total, apart, apart2, m2, var = (ln_tmp[:, c, :] for c in range(5))
                if part == 0:
                    dve.wait_ge(stat_sem, n * GT + GT)
                    tt(total, mean_e, mean_o, ALU.add).then_inc(var_sem, 1)
                    tt(apart, mean_e, mean_o, ALU.subtract).then_inc(var_sem, 1)
                    tt(m2, m2_e, m2_o, ALU.add).then_inc(var_sem, 1)
                    dve.wait_ge(var_sem, n * LN_VAR + 3)
                    ts(mean_out[:], total, -0.5 if mean_out is neg_mean else 0.5, None, ALU.mult).then_inc(var_sem, 1)
                    stt(out=apart2, in0=apart, scalar=0.25, in1=apart, op0=ALU.mult, op1=ALU.mult).then_inc(var_sem, 1)
                    ts(var, m2, 1.0 / H, LN_EPS, ALU.mult, ALU.add).then_inc(var_sem, 1)
                else:
                    dve.wait_ge(var_sem, n * LN_VAR + 6)
                    tt(var_eps[:], var, apart2, ALU.add).then_inc(var_sem, 1)

            def ffn(ph):
                base, groups = ph * NG * STEPS, ph * NG

                def prep_stats(g, half):
                    if ph == 0 and isinstance(g, int) and half == 0:
                        dve.wait_ge(in_x[g], 16)
                    if ph == 1 and half == 0:
                        dve.wait_ge(x_attended, g + 1)
                    moments(of_group(x, g), ln_stat, (2 * half, 2 * half + 1))

                def prep_var(g, part):
                    variance_part(g + 2 * groups, ln_stat, ln_var, neg_mean, part)

                def prep_stats2(g, half):
                    dve.wait_ge(ln_done, g + (2 * groups + 1))
                    moments(z[:].rearrange("p t f -> p (t f)"), ln_stat2, (2 * half, 2 * half + 1))

                def prep_var2(g, part):
                    variance_part(g + groups, ln_stat2, ln_var2, mean2, part)

                def prep_route(g, part, by_exp=False):
                    n = g + groups

                    def done(ins):
                        ins.then_inc(rt_step, 1)

                    def after(step):
                        dve.wait_ge(rt_step, n * RT + step)

                    of_f = r_b[:].unsqueeze(2).broadcast_to([P, GT, NE, NE])
                    of_e = r_b[:].unsqueeze(3).broadcast_to([P, GT, NE, NE])

                    if part == 0:
                        logits = psum[:, R_BANK, 0:GT * NE].rearrange("p (t e) -> p t e", t=GT)
                        dve.wait_ge(logits_ready, n + 1)
                        done(tt(r_a[:], gate_sum[:, 0, :].unsqueeze(1).broadcast_to([P, GT, NE]), spread(mean2[:], NE), ALU.mult))
                        after(1)
                        done(tt(r_b[:], logits, r_a[:], ALU.subtract))
                    elif part == 1:
                        dve.wait_ge(ln_rstd2, n + 1)
                        after(2)
                        done(tt(r_a[:], r_b[:], spread(rstd2[:], NE), ALU.mult))
                        after(3)
                        done(tt(r_b[:], r_a[:], gate_sum[:, 1, :].unsqueeze(1).broadcast_to([P, GT, NE]), ALU.add))
                    elif part == 2:
                        after(4)
                        done(nc.vector.tensor_reduce(r_1[:], r_b[:], AX.X, ALU.max))
                        after(5)
                        done(tt(r_a[:], r_b[:], spread(r_1[:], NE), ALU.subtract))
                    elif part == 3:
                        after(6)
                        done(ts(r_c[:], r_a[:], -1.0, None, ALU.add))
                        after(7)
                        if not by_exp:
                            done(nc.vector.reciprocal(r_a[:], r_c[:]))
                    elif part == 4 and by_exp:
                        dve.wait_ge(rt_silu, n + 1)
                        cp(r_a[:], r_silu[:]).then_inc(rt_step, 5)
                    elif part == 5 and by_exp:
                        pass
                    elif part == 4:
                        after(8)
                        dve.wait_ge(rt_silu, n + 1)
                        done(tt(r_b[:], r_silu[:], r_a[:], ALU.mult))
                        after(9)
                        done(ts(r_a[:], r_b[:], -1.0, 1.0, ALU.mult, ALU.add))
                    elif part == 5:
                        after(10)
                        done(nc.vector.reciprocal(r_c[:], r_a[:]))
                        after(11)
                        done(tt(r_a[:], r_b[:], r_c[:], ALU.mult))
                    elif part == 6:
                        after(12)
                        done(nc.vector.tensor_reduce(r_2[:], r_a[:], AX.X, ALU.add))
                        after(13)
                        done(nc.vector.reciprocal(r_3[:], r_2[:]))
                    elif part == 7:
                        after(14)
                        done(tt(r_b[:], r_a[:], spread(r_3[:], NE), ALU.mult))
                        after(15)
                        done(tt(r_gt[:], of_f, of_e, ALU.is_gt))
                    elif part == 8:
                        done(tt(r_eq[:], of_f, of_e, ALU.is_equal))
                        after(17)
                        done(tt(r_eq[:], r_eq[:], lower[:].unsqueeze(1).broadcast_to([P, GT, NE, NE]), ALU.mult))
                    elif part == 9:
                        after(18)
                        done(tt(r_gt[:], r_gt[:], r_eq[:], ALU.add))
                        after(19)
                        done(nc.vector.tensor_reduce(r_a[:], r_gt[:], AX.X, ALU.add))
                    elif part == 10:
                        after(20)
                        done(stt(out=r_c[:], in0=r_a[:], scalar=float(TOPK), in1=r_b[:], op0=ALU.is_lt, op1=ALU.mult))
                        after(21)
                        done(nc.vector.tensor_reduce(r_1[:], r_c[:], AX.X, ALU.add))
                    elif part == 11:
                        after(22)
                        done(ts(r_2[:], r_1[:], TOPK_EPS, None, ALU.add))
                        after(23)
                        done(nc.vector.reciprocal(r_3[:], r_2[:]))
                    elif part == 12:
                        after(24)
                        done(tt(r_a[:], r_c[:], spread(r_3[:], NE), ALU.mult))
                    elif part == 13:
                        dve.wait_ge(route_turned, n)
                        after(25)
                        done(cp(route[:, :, 0:NE], r_a[:]))
                        after(26)
                        done(tt(route[:, :, 32:32 + NE], r_a[:], route[:, :, 0:NE].bitcast(F32), ALU.subtract))

                def prepare(g, place):
                    if place - AT_STATS in (0, 1):
                        prep_stats(g, place - AT_STATS)
                    if place - AT_VAR in (0, 1):
                        prep_var(g, place - AT_VAR)
                    if place - AT_STATS2 in (0, 1):
                        prep_stats2(g, place - AT_STATS2)
                    if place - AT_VAR2 in (0, 1):
                        prep_var2(g, place - AT_VAR2)
                    if 0 <= place - AT_ROUTE < ROUTE_PARTS:
                        prep_route(g, place - AT_ROUTE)

                def product(g, s, between):
                    n = g * STEPS + (s + base)
                    dve.wait_ge(up_ready, n + 1)
                    dve.wait_ge(silu_ready, n + 1)
                    if not (ph == 0 and is_first(g) and s < LAG):
                        dve.wait_ge(lo_ready, n - (LAG - 1))
                    if s < 2:
                        tt(h[:, s % LAG, :], silu[:, s % 2, :], bank(U_BANK[s % 2]), ALU.mult).then_inc(up_used, 1)
                        between()
                    else:
                        dve.wait_ge(h_ready, g * (2 * NE) + (groups * 2 * NE + s - 2))
                        tt(act_up[:], silu[:, s % 2, :], bank(U_BANK[s % 2]), ALU.mult).then_inc(up_used, 1)
                        between()
                        dve.wait_ge(bc_ready, g * NE + (groups * NE + s // 2))
                        dve.wait_ge(up_used, n + 1)
                        tt(h[:, s % LAG, :], act_up[:], bank(BC_BANK), ALU.mult).then_inc(h_ready, 1)

                def update(g, last_group):
                    dve.wait_ge(out_turned, g + groups + 1)
                    stt(out=of_group(x, g), in0=bank(BC_BANK if last_group else Z_BANK), scalar=0.5, in1=of_group(x, g),
                        op0=ALU.mult, op1=ALU.add).then_inc(x_updated, 1)

                def window(g, k0, k1, last):
                    for k in range(k0, k1):
                        if last and ph == 0:
                            attend(0, beside.get(k - 1, []))
                        def between():
                            if not last:
                                prepare(g + 1, 2 * k)

                        product(*group_step(g, k), between)
                        if not last:
                            prepare(g + 1, 2 * k + 1)
                        if ph == 0 and is_first(g):
                            if expert_at(k) is not None:
                                split_expert(expert_at(k))
                            if k == AT_VALUES + 1:
                                add_bias()
                            if 0 <= k - AT_PARTS < HI:
                                split_keys(k - AT_PARTS)
                            if k == AT_PARTS + HI:
                                split_queries()
                            if k == PRE + STEPS - 1:
                                for x_g in range(2, NG):
                                    dve.wait_ge(in_x[x_g], 16)
                        if ph == 1 and k == 1:
                            reciprocals(NG - 1)
                        if not last:
                            if k == AT_UPDATE:
                                update(g, False)
                    if last:
                        if ph == 0:
                            for k in range(STEPS - 1, STEPS + LAG):
                                attend(0, beside.get(k, []))
                        update(g, True)

                def open_route():
                    for part in range(ROUTE_PARTS):
                        prep_route(0, part, ph == 1)

                def open_stats():
                    for part in range(2):
                        prep_stats(0, part)
                    for part in range(2):
                        prep_var(0, part)

                def open_stats2():
                    for part in range(2):
                        prep_stats2(0, part)
                    for part in range(2):
                        prep_var2(0, part)

                return {"stats": open_stats, "stats2": open_stats2, "route": open_route, "run": lambda: ffn_windows(dve, window, ph)}

            first, second = ffn(0), ffn(1)

            def split_expert(e):
                dve.wait_ge(w_rounded, e + 1)
                tt(w_lo[:, e, :], w_raw[:, e % RAW, :], w_hi[:, e, :].bitcast(F32), ALU.subtract).then_inc(w_split, 1)

            def split_keys(i):
                dve.wait_ge(k_ready, 2 * i + 2)
                tt(k_parts[32:64, i, :], k_fp[32:64, i, :], k_parts[32:64, i, :].bitcast(F32), ALU.subtract).then_inc(k_split, 1)

            def add_bias():
                dve.wait_ge(in_k, IN_K)
                dve.wait_ge(v_projected, 1)
                tt(v_fp, bank(Z_BANK).rearrange("p (k c) -> p k c", k=KB), bv[:].unsqueeze(1).broadcast_to([P, KB, H]),
                   ALU.add).then_inc(v_ready, 1)

            def split_queries():
                cp(wq_hi[:], wq_raw).then_inc(wq_rounded, 1)
                dve.wait_ge(wq_rounded, 1)
                tt(wq_lo[:], wq_raw, wq_hi[:].bitcast(F32), ALU.subtract).then_inc(wq_split, 1)

            def reciprocals(g):
                dve.wait_ge(den_placed, g * DEN_MOVES + DEN_MOVES)
                nc.vector.reciprocal(den_c[:], den_c[:]).then_inc(recip_done, 1)

            first["stats"]()
            dve.wait_ge(in_g, IN_G)
            ts(gate_s[:, 0, :], gate_t[:], ln_scale[:], None, ALU.mult).then_inc(gates_scaled, 1)
            ts(gate_s[:, 1, :], gate_t[:], ln_bias[:], None, ALU.mult).then_inc(gates_scaled, 1)
            split_expert(0)
            dve.wait_ge(gates_summed, 1)
            cp(gate_sum[:].rearrange("p a e -> p (a e)"), psum[:, GS_BANK, 0:2 * NE]).then_inc(sums_read, 1)
            first["stats2"]()
            split_expert(1)
            dve.wait_ge(sums_read, 1)
            dve.wait_ge(in_c, IN_C)
            first["route"]()

            def attend(g0, events):
                mt_use, _ = ring_uses(events)
                for ev in events:
                    kind = ev[0]
                    if kind == "NEXT" and ev[1] in second:
                        second[ev[1]]()
                    if kind == "M":
                        _, u, qt, j = ev
                        r = 16 * u + 4 * qt + j
                        dve.wait_ge(m_filled, g0 * 64 + (r + 1))
                        b, _ = m_bank(r, is_first(g0))
                        nc.vector.tensor_reduce(neg_max[:, u % 2, qt, j:j + 1], bank(b), AX.X, ALU.max,
                                                negate=True).then_inc(m_freed, 1)
                        if qt == GT - 1 and j == HJ - 1:
                            dve.wait_ge(m_freed, g0 * 64 + 16 * (u + 1))
                            if u >= 1:
                                dve.wait_ge(s_filled, g0 * RING + (RING0 + mt_use[u - 1] + 1))
                            cp(max_stage[:, :, QROWS:QROWS + HJ], neg_max[:, u % 2]).then_inc(max_hi, 1)
                            dve.wait_ge(max_hi, g0 * HI + (u + 1))
                            tt(max_stage[:, :, QROWS + HJ:QROWS + 2 * HJ], neg_max[:, u % 2],
                               max_stage[:, :, QROWS:QROWS + HJ].bitcast(F32), ALU.subtract).then_inc(max_lo, 1)
                    elif kind == "LNS":
                        _, dg, part = ev
                        if part < 2:
                            moments(of_group(x, g0 + dg), ln_stat, (2 * part, 2 * part + 1))
                        else:
                            variance_part(g0 + (dg + NG), ln_stat, ln_var, neg_mean, part - 2)
                    elif kind == "RECIP":
                        reciprocals(g0 + ev[1])

            first["run"]()
            att_windows(dve, attend)
            second["run"]()

        @block.gpsimd
        def _(pool):
            nc.gpsimd.memset(minus_half[:], -0.5).then_inc(pool_set, 1)
            nc.gpsimd.memset(route[:].bitcast(F32), 0.0).then_inc(pool_set, 1)
            nc.gpsimd.memset(max_stage[:].bitcast(F32), 0.0).then_inc(pool_set, 1)
            nc.gpsimd.memset(v_pad[:], 0.0).then_inc(pool_set, 1)
            pool.wait_ge(pool_set, 4)
            for i in range(HI):
                c = 2 * DH + DH * (i % 2)
                nc.gpsimd.memset(v_pad[:, :, i, :, c:c + DH], 1.0).then_inc(pool_set, 1)
            pool.wait_ge(pool_set, POOL_SETS)

            def inverse_root(n, var_sem, out, out_sem):
                pool.wait_ge(var_sem, n * LN_VAR + LN_VAR)
                nc.gpsimd.tensor_tensor(out[:], var_eps[:], minus_half[:], ALU.pow).then_inc(out_sem, 1)

            def deviation(n):
                inverse_root(n, ln_var, rstd, ln_rstd)
                pool.wait_ge(ln_rstd, n + 1)
                nc.gpsimd.tensor_tensor(shift[:], neg_mean[:], rstd[:], ALU.mult).then_inc(ln_shift, 1)

            def ffn(ph):
                base, groups = ph * NG * STEPS, ph * NG

                def prep_stats(g):
                    deviation(g + 2 * groups)

                def prep_norm(g):
                    inverse_root(g + groups, ln_var2, rstd2, ln_rstd2)

                def prep_split(g):
                    pool.wait_ge(z_rounded, g + groups + 1)
                    pool.wait_ge(z_copied, g + groups + 1)
                    nc.gpsimd.tensor_tensor(of_group(zT_lo, g % 2), zT[:], of_group(zT_hi, g % 2).bitcast(F32),
                                            ALU.subtract).then_inc(z_split, 1)

                def split_h(g, s):
                    n = g * STEPS + (s + base)
                    pool.wait_ge(hi_ready, n + 1)
                    nc.gpsimd.tensor_tensor(h_lo[:, s % LAG, :], h[:, s % LAG, :], h_hi[:, s % LAG, :].bitcast(F32),
                                            ALU.subtract).then_inc(lo_ready, 1)

                def window(g, k0, k1, last):
                    for k in range(k0, k1):
                        if last and ph == 0:
                            attend(0, beside.get(k - 1, []))
                        if k >= 1:
                            split_h(*group_step(g, k - 1))
                        if not last:
                            if k == AT_RSTD:
                                prep_stats(g + 1)
                            if k == AT_SPLIT:
                                prep_split(g + 1)
                            if k == AT_RSTD2:
                                prep_norm(g + 1)
                        if ph == 1 and k == PRE - 2:
                            post(NG - 1, 0)
                        if ph == 1 and k == PRE - 1:
                            post(NG - 1, 1)
                    if last:
                        split_h(g, STEPS - 1)

                return {"stats": lambda: prep_stats(0), "stats2": lambda: prep_norm(0), "split": lambda: prep_split(0),
                        "run": lambda: ffn_windows(pool, window, ph)}

            first, second = ffn(0), ffn(1)

            def attend(g0, events):
                for ev in events:
                    kind, use = ev[0], ev[-1]
                    if kind == "NEXT" and ev[1] in second:
                        second[ev[1]]()
                    if kind == "POST":
                        post(g0 + ev[1], 0)
                        post(g0 + ev[1], 1)
                    elif kind == "LNS" and ev[2] == 3:
                        deviation(g0 + (ev[1] + NG))
                    elif kind == "PROJ":
                        u = ev[1]
                        i = u % HI
                        pool.wait_ge(s_freed, g0 * RING + (RING0 + use + 1))
                        pool.wait_ge(q_rounded, g0 * HI + (u + 1))
                        nc.gpsimd.tensor_tensor(q_stack[0:32, i, :], q_fp[:, u % 2, :],
                                                q_stack[0:32, i, :].bitcast(F32), ALU.subtract).then_inc(q_ready, 1)
                    elif kind == "YT":
                        g, half = g0 + ev[1], ev[2]
                        cols = slice(2 * half * P, 2 * (half + 1) * P)
                        pool.wait_ge(s_freed, g0 * RING + (RING0 + use + 1))
                        pool.wait_ge(y_rounded, 2 * g + (half + 1))
                        nc.gpsimd.tensor_tensor(yT_lo[:, cols], zT[:, cols], yT_hi[:, cols].bitcast(F32),
                                                ALU.subtract).then_inc(y_split, 1)
                        if half == 1:
                            nc.gpsimd.tensor_tensor(of_group(x, g), of_group(x, g), z[:].rearrange("p t f -> p (t f)"),
                                                    ALU.add).then_inc(y_added, 1)

            def post(g, part):
                if part == 0:
                    pool.wait_ge(rden_placed, g * (16 * HJ) + 16 * HJ)
                    pool.wait_ge(num_placed, g * NUM_MOVES + NUM_MOVES)
                    nc.gpsimd.tensor_tensor(num, num, rden, ALU.mult).then_inc(att_done, 1)
                    return
                pool.wait_ge(att_done, g + 1)
                pool.wait_ge(y_added, g + 1)
                for t in range(2):
                    xs = of_group(x, g).rearrange("p (b k t) -> p b k t", b=2, t=2)[:, :, :, t]
                    last = nc.gpsimd.tensor_tensor(xs, xs, num.rearrange("p (b t k) -> p b t k", b=2, t=2)[:, :, t, :], ALU.add)
                last.then_inc(x_attended, 1)

            first["stats"]()
            pool.wait_ge(in_c, IN_C)
            pool.wait_ge(ones_set, 1)
            nc.gpsimd.tensor_tensor(expert_sel[:], expert_ind[:].unsqueeze(2).broadcast_to([P, NE, P]),
                                    ones[:].unsqueeze(1).broadcast_to([P, NE, P]), ALU.mult).then_inc(sel_set, 1)
            first["stats2"]()
            first["split"]()
            nc.gpsimd.memset(k_parts[:].bitcast(F32), 1.0).then_inc(k_split, 1)
            first["run"]()
            att_windows(pool, attend)
            second["run"]()


def kernel(L0_attn_queries, L0_attn_keys, L0_attn_values, L0_attn_Wq_w, L0_attn_Wq_b, L0_attn_Wk_w, L0_attn_Wk_b,
           L0_attn_Wv_w, L0_attn_Wv_b, L0_ffn_ln_scale, L0_ffn_ln_bias, L0_ffn_gate_w, L0_ffn_Wg, L0_ffn_Wu, L0_ffn_Wd,
           L0_ffn_sWg, L0_ffn_sWu, L0_ffn_sWd):
    import concourse.bacc as bacc
    from concourse.bass_utils import run_bass_kernel_spmd

    f32 = np.float32

    def arr(a):
        return np.ascontiguousarray(np.asarray(a))

    def stack_weights(w):
        w = arr(w).T.reshape(H, HJ, HI, DH).transpose(0, 2, 1, 3).reshape(H, HI, 1, HJ * DH)
        return np.ascontiguousarray(np.repeat(w, 3, axis=2).reshape(H, HI * QROWS))

    def stack_bias(b):
        b = arr(b).reshape(HJ, HI, DH).transpose(0, 2, 1).reshape(HJ * DH, HI)
        return np.ascontiguousarray(np.tile(b, (3, 1)))

    p = np.arange(P)
    copies = p[:, None] < QROWS
    head = np.where(copies, (p[:, None] % 32) // DH == np.arange(HJ), (p[:, None] - QROWS) % HJ == np.arange(HJ))
    head = head & (p[:, None] < QROWS + 2 * HJ)
    expert = (p[:, None] == np.arange(NE)) | (p[:, None] == 32 + np.arange(NE))
    lower = np.arange(NE)[None, :] < np.arange(NE)[:, None]
    arrays = {
        "x": arr(L0_attn_queries), "keysT": arr(arr(L0_attn_keys)[0].T), "valuesT": arr(arr(L0_attn_values)[0].T),
        "wq": stack_weights(L0_attn_Wq_w), "wk": stack_weights(L0_attn_Wk_w), "wvT": arr(arr(L0_attn_Wv_w).T),
        "bq": stack_bias(L0_attn_Wq_b), "bk": stack_bias(L0_attn_Wk_b),
        "bv": np.ascontiguousarray(np.tile(arr(L0_attn_Wv_b)[None, :], (P, 1))),
        "ln_scale": arr(L0_ffn_ln_scale).reshape(H, 1), "ln_bias": arr(L0_ffn_ln_bias).reshape(H, 1),
        "gate_t": arr(arr(L0_ffn_gate_w).T), "Wg": arr(L0_ffn_Wg), "Wu": arr(L0_ffn_Wu), "Wd": arr(L0_ffn_Wd),
        "sWg": arr(L0_ffn_sWg), "sWu": arr(L0_ffn_sWu), "sWd": arr(L0_ffn_sWd),
        "c_ident": np.eye(P, dtype=f32), "c_head": head.astype(f32), "c_expert": expert.astype(f32),
        "c_lower": np.ascontiguousarray(np.broadcast_to(lower.reshape(1, NE * NE), (P, NE * NE)).astype(f32)),
    }
    nc = bacc.Bacc("TRN2", target_bir_lowering=False, num_devices=1)
    d = {n: nc.dram_tensor(f"in_{n}", a.shape, mybir.dt.from_np(a.dtype), kind="ExternalInput").ap() for n, a in arrays.items()}
    d["out"] = nc.dram_tensor("out_x", (NB, S, H), F32, kind="ExternalOutput").ap()
    d["recip"] = nc.dram_tensor("recip", (HI, HJ, GTOK), F32).ap()
    build(nc, d)
    r = run_bass_kernel_spmd(nc, [{f"in_{n}": a for n, a in arrays.items()}], core_ids=[0])
    return r.results[0]["out_x"]
```
